# Optimizing a Trainium2 kernel written in Bass

```python
import numpy as np
import jax
import jax.numpy as jnp

def _softmax(x, axis=-1):
    return jax.nn.softmax(x, axis=axis)

def _gelu(x):
    return jax.nn.gelu(x, approximate=True)

def _silu(x):
    return jax.nn.silu(x)

def _sigmoid(x):
    return jax.nn.sigmoid(x)

def _layernorm(x, axis=-1, eps=1e-05):
    m = jnp.mean(x, axis=axis, keepdims=True)
    v = jnp.var(x, axis=axis, keepdims=True)
    return (x - m) / jnp.sqrt(v + eps)

def _scatter_add(tgt, idx, src, axis=0):
    return tgt.at[idx].add(src)

def _segment_sum(src, seg, n):
    return jax.ops.segment_sum(src, seg, n)
kernel_name = 'mk_decoder_postln_d1_seqx_r8_e68dd3'

def setup_inputs(seed: int=0):
    np.random.seed(seed)
    _w = jnp.asarray

    def _rec_inputs():
        import jax
        import jax.numpy as jnp
        _rk = jax.random.key(seed)
        x = 7.22e-05 + 1 * jax.random.normal(jax.random.fold_in(_rk, 1), (4, 512, 128), jnp.float32)
        _lenS = 512 - jax.random.randint(jax.random.fold_in(_rk, 7), (4,), 0, max(1, 512 // 4) + 1, jnp.int32)
        _lenS2 = 77 - jax.random.randint(jax.random.fold_in(_rk, 8), (4,), 0, max(1, 77 // 4) + 1, jnp.int32)
        _ctx_1024P = jax.random.normal(jax.random.fold_in(_rk, 11), (4, 16, 128), jnp.float32)
        _ctx_1024c = jax.random.dirichlet(jax.random.fold_in(_rk, 511), 0.3 * jnp.ones((16,), jnp.float32), (4, 77))
        _ctx_1024t = jnp.einsum('bsk,bkd->bsd', _ctx_1024c, _ctx_1024P)
        _ctx_1024t = _ctx_1024t * jax.lax.rsqrt(jnp.mean(jnp.square(_ctx_1024t)) + 1e-12) * 0.953939
        ctx_1024 = 4.13588e-05 + 0.999923 * (_ctx_1024t + 0.3 * jax.random.normal(jax.random.fold_in(_rk, 611), (4, 77, 128), jnp.float32))
        return (x, ctx_1024)
    x, ctx_1024 = _rec_inputs()

    def _L0_attn_setup():
        import jax, jax.numpy as jnp
        import numpy as np
        B, T, C = (4, 256, 128)
        NQ, D = (8, C // 8)
        key = jax.random.key(seed)
        ks = jax.random.split(key, 6)
        s = 0.02
        return {'x': jax.random.normal(ks[0], (B, T, C), dtype=jnp.float32), 'Wk': jax.random.normal(ks[1], (C, D), dtype=jnp.float32) * s, 'Wv': jax.random.normal(ks[2], (C, D), dtype=jnp.float32) * s, 'Wq': jax.random.normal(ks[3], (NQ, C, D), dtype=jnp.float32) * s, 'Wp': jax.random.normal(ks[4], (NQ * D, C), dtype=jnp.float32) * s, 'bp': jnp.zeros((C,), dtype=jnp.float32)}
    _L0_attn_all = _L0_attn_setup()
    _L0_attn_in = {k: v for k, v in _L0_attn_all.items() if k in ('Wk', 'Wv', 'Wq', 'Wp', 'bp')}
    del _L0_attn_all

    def _L0_xattn_setup():
        import math
        import jax, jax.numpy as jnp
        import numpy as np
        H = 16
        D_MODEL = 128
        DK = D_MODEL // H
        K_FACTOR = 2

        def _time_delay_agg_inference(v, corr):
            B, _, _, L = v.shape
            top_k = min(int(K_FACTOR * math.log(L)), L)
            mean_value = jnp.mean(corr, axis=(1, 2))
            weights, delay = jax.lax.top_k(mean_value, top_k)
            tmp_corr = jax.nn.softmax(weights, axis=-1)
            idx = (delay[:, :, None] + jnp.arange(L)) % L
            gathered = jnp.take_along_axis(v[:, None], idx[:, :, None, None, :], axis=-1)
            return jnp.einsum('bk,bkhdl->bhdl', tmp_corr, gathered)
        key = jax.random.key(seed)
        ks = jax.random.split(key, 11)
        B, L, D = (4, 256, D_MODEL)
        s = 1.0 / math.sqrt(D)
        return {'queries': jax.random.normal(ks[0], (B, L, D), jnp.float32), 'keys': jax.random.normal(ks[1], (B, L, D), jnp.float32), 'values': jax.random.normal(ks[2], (B, L, D), jnp.float32), 'Wq': jax.random.normal(ks[3], (D, H * DK), jnp.float32) * s, 'bq': jnp.zeros((H * DK,), jnp.float32), 'Wk': jax.random.normal(ks[4], (D, H * DK), jnp.float32) * s, 'bk': jnp.zeros((H * DK,), jnp.float32), 'Wv': jax.random.normal(ks[5], (D, H * DK), jnp.float32) * s, 'bv': jnp.zeros((H * DK,), jnp.float32), 'Wo': jax.random.normal(ks[6], (H * DK, D), jnp.float32) * s, 'bo': jnp.zeros((D,), jnp.float32)}
    _L0_xattn_all = _L0_xattn_setup()
    _L0_xattn_in = {k: v for k, v in _L0_xattn_all.items() if k in ('Wq', 'bq', 'Wk', 'bk', 'Wv', 'bv', 'Wo', 'bo')}
    del _L0_xattn_all

    def _L0_ffn_setup():
        import jax, jax.numpy as jnp
        import numpy as np
        BLOCK = 32
        W_BITS = 4
        ACT_BITS = 16

        def act_qdq(x):
            qmax = 2.0 ** (ACT_BITS - 1) - 1.0
            scale = jnp.maximum(jnp.max(jnp.abs(x)) / qmax, 1e-12)
            return jnp.clip(jnp.round(x / scale), -qmax - 1.0, qmax) * scale

        def fixed_qdq_u16(x):
            scale = 1.0 / 65536.0
            return jnp.clip(jnp.round(x / scale), 0.0, 65535.0) * scale

        def lpbq_dequant(w):
            O, I = w.shape
            qmax = 2.0 ** (W_BITS - 1) - 1.0
            wb = w.reshape(O, I // BLOCK, BLOCK)
            s = jnp.maximum(jnp.max(jnp.abs(wb), axis=-1, keepdims=True) / qmax, 1e-12)
            wq = jnp.clip(jnp.round(wb / s), -qmax - 1.0, qmax) * s
            return wq.reshape(O, I)
        key = jax.random.key(seed)
        k1, k2, k3, k4 = jax.random.split(key, 4)
        B, S, H, I = (2, 512, 128, 384)
        x = jax.random.normal(k1, (B, S, H), jnp.float32)
        w_gate = jax.random.normal(k2, (I, H), jnp.float32) * 0.02
        w_up = jax.random.normal(k3, (I, H), jnp.float32) * 0.02
        w_down = jax.random.normal(k4, (H, I), jnp.float32) * 0.02
        return {'x': x, 'w_gate': w_gate, 'w_up': w_up, 'w_down': w_down}
    _L0_ffn_all = _L0_ffn_setup()
    _L0_ffn_in = {k: v for k, v in _L0_ffn_all.items() if k in ('w_gate', 'w_up', 'w_down')}
    del _L0_ffn_all
    return {'x': x, 'ctx_1024': ctx_1024, 'L0_attn_Wk': _L0_attn_in['Wk'], 'L0_attn_Wv': _L0_attn_in['Wv'], 'L0_attn_Wq': _L0_attn_in['Wq'], 'L0_attn_Wp': _L0_attn_in['Wp'], 'L0_attn_bp': _L0_attn_in['bp'], 'L0_xattn_Wq': _L0_xattn_in['Wq'], 'L0_xattn_bq': _L0_xattn_in['bq'], 'L0_xattn_Wk': _L0_xattn_in['Wk'], 'L0_xattn_bk': _L0_xattn_in['bk'], 'L0_xattn_Wv': _L0_xattn_in['Wv'], 'L0_xattn_bv': _L0_xattn_in['bv'], 'L0_xattn_Wo': _L0_xattn_in['Wo'], 'L0_xattn_bo': _L0_xattn_in['bo'], 'L0_ffn_w_gate': _L0_ffn_in['w_gate'], 'L0_ffn_w_up': _L0_ffn_in['w_up'], 'L0_ffn_w_down': _L0_ffn_in['w_down']}

def reference(x, ctx_1024, L0_attn_Wk, L0_attn_Wv, L0_attn_Wq, L0_attn_Wp, L0_attn_bp, L0_xattn_Wq, L0_xattn_bq, L0_xattn_Wk, L0_xattn_bk, L0_xattn_Wv, L0_xattn_bv, L0_xattn_Wo, L0_xattn_bo, L0_ffn_w_gate, L0_ffn_w_up, L0_ffn_w_down):
    import jax
    import jax.numpy as jnp

    def _L0_attn_ref(x, Wk, Wv, Wq, Wp, bp):
        import jax, jax.numpy as jnp
        import numpy as np
        B, T, C = (4, 256, 128)
        NQ, D = (8, C // 8)
        b, t, c = x.shape
        scale = c ** (-0.5)
        k = x @ Wk
        v = x @ Wv
        q = jnp.einsum('btc,qcd->bqtd', x, Wq)
        wei = jnp.einsum('bqtd,bsd->bqts', q, k) * scale
        causal = jnp.tril(jnp.ones((t, t), dtype=bool))
        wei = jnp.where(causal, wei, -jnp.inf)
        wei = jax.nn.softmax(wei, axis=-1)
        out = jnp.einsum('bqts,bsd->btqd', wei, v)
        out = out.reshape(b, t, -1)
        return out @ Wp + bp

    def _L0_xattn_ref(queries, keys, values, Wq, bq, Wk, bk, Wv, bv, Wo, bo):
        import math
        import jax, jax.numpy as jnp
        import numpy as np
        H = 16
        D_MODEL = 128
        DK = D_MODEL // H
        K_FACTOR = 2

        def _time_delay_agg_inference(v, corr):
            B, _, _, L = v.shape
            top_k = min(int(K_FACTOR * math.log(L)), L)
            mean_value = jnp.mean(corr, axis=(1, 2))
            weights, delay = jax.lax.top_k(mean_value, top_k)
            tmp_corr = jax.nn.softmax(weights, axis=-1)
            idx = (delay[:, :, None] + jnp.arange(L)) % L
            gathered = jnp.take_along_axis(v[:, None], idx[:, :, None, None, :], axis=-1)
            return jnp.einsum('bk,bkhdl->bhdl', tmp_corr, gathered)
        B, Lq, _ = queries.shape
        Lk = keys.shape[1]
        q = (queries @ Wq + bq).reshape(B, Lq, H, DK)
        k = (keys @ Wk + bk).reshape(B, Lk, H, DK)
        v = (values @ Wv + bv).reshape(B, Lk, H, DK)
        if Lq > Lk:
            pad = ((0, 0), (0, Lq - Lk), (0, 0), (0, 0))
            k = jnp.pad(k, pad)
            v = jnp.pad(v, pad)
        else:
            k = k[:, :Lq]
            v = v[:, :Lq]
        qt = jnp.transpose(q, (0, 2, 3, 1))
        kt = jnp.transpose(k, (0, 2, 3, 1))
        vt = jnp.transpose(v, (0, 2, 3, 1))
        qf = jnp.fft.rfft(qt)
        kf = jnp.fft.rfft(kt)
        c = qf.real * kf.real + 1j * -(qf.imag * kf.imag)
        corr = jnp.fft.irfft(c, n=Lq).astype(qt.dtype)
        agg = _time_delay_agg_inference(vt, corr)
        out = jnp.transpose(agg, (0, 3, 1, 2)).reshape(B, Lq, H * DK)
        return out @ Wo + bo

    def _L0_ffn_ref(x, w_gate, w_up, w_down):
        import jax, jax.numpy as jnp
        import numpy as np
        BLOCK = 32
        W_BITS = 4
        ACT_BITS = 16

        def act_qdq(x):
            qmax = 2.0 ** (ACT_BITS - 1) - 1.0
            scale = jnp.maximum(jnp.max(jnp.abs(x)) / qmax, 1e-12)
            return jnp.clip(jnp.round(x / scale), -qmax - 1.0, qmax) * scale

        def fixed_qdq_u16(x):
            scale = 1.0 / 65536.0
            return jnp.clip(jnp.round(x / scale), 0.0, 65535.0) * scale

        def lpbq_dequant(w):
            O, I = w.shape
            qmax = 2.0 ** (W_BITS - 1) - 1.0
            wb = w.reshape(O, I // BLOCK, BLOCK)
            s = jnp.maximum(jnp.max(jnp.abs(wb), axis=-1, keepdims=True) / qmax, 1e-12)
            wq = jnp.clip(jnp.round(wb / s), -qmax - 1.0, qmax) * s
            return wq.reshape(O, I)
        x = act_qdq(x)
        up = act_qdq(x @ lpbq_dequant(w_up).T)
        gate = act_qdq(x @ lpbq_dequant(w_gate).T)
        sig = fixed_qdq_u16(jax.nn.sigmoid(gate))
        gate = act_qdq(gate * sig)
        o = act_qdq(gate * up)
        return o @ lpbq_dequant(w_down).T
    x = _layernorm(x + _L0_attn_ref(x, L0_attn_Wk, L0_attn_Wv, L0_attn_Wq, L0_attn_Wp, L0_attn_bp), axis=-1)
    x = _layernorm(x + _L0_xattn_ref(x, ctx_1024, ctx_1024, L0_xattn_Wq, L0_xattn_bq, L0_xattn_Wk, L0_xattn_bk, L0_xattn_Wv, L0_xattn_bv, L0_xattn_Wo, L0_xattn_bo), axis=-1)
    x = _layernorm(x + _L0_ffn_ref(x, L0_ffn_w_gate, L0_ffn_w_up, L0_ffn_w_down), axis=-1)
    return x

_drawn_inputs = setup_inputs


def setup_inputs(seed=0):
    import zlib

    import numpy as np

    out = dict(_drawn_inputs(seed))
    spreads = {'L0_attn_bp': (0.0, 0.1),
     'L0_xattn_bq': (0.0, 0.8),
     'L0_xattn_bk': (0.0, 0.1),
     'L0_xattn_bv': (0.0, 0.407),
     'L0_xattn_bo': (0.0, 0.1)}
    factors = {'L0_attn_Wk': 8.0,
     'L0_attn_Wv': 8.0,
     'L0_attn_Wq': 8.0,
     'L0_attn_Wp': 8.0,
     'L0_ffn_w_gate': 5.274,
     'L0_ffn_w_up': 4.972,
     'L0_ffn_w_down': 5.037}
    for name, (base, spread) in spreads.items():
        noise = np.random.default_rng([zlib.crc32(name.encode()), seed]).standard_normal(out[name].shape)
        drawn = base * np.exp(spread * noise) if base else spread * noise
        out[name] = jnp.asarray(drawn.astype(out[name].dtype))
    for name, factor in factors.items():
        out[name] = (out[name] * factor).astype(out[name].dtype)
    return out
```

```python
from contextlib import ExitStack

import numpy as np

import concourse.bass as bass
from concourse import mybir

F32 = mybir.dt.float32
BF16 = mybir.dt.bfloat16
I16 = mybir.dt.int16
U16 = mybir.dt.uint16
ALU = mybir.AluOpType
ACT = mybir.ActivationFunctionType
AX = mybir.AxisListType

P = 128
B, T, C = 4, 512, 128
NT = T // P
NH, D = 8, 16
S2 = 77
I = 384
NI = I // P
BLK = 32
NB = C // BLK * NI
TOPK = int(2 * np.log(T))
SCALE = C ** -0.5
EPS = 1e-5
QMAX = 32767.0
MAGIC = 1.5 * 2.0 ** 23
LOWEST = -3.0e38
Q_PART = [0, 0, 0, 1, 1, 2]
K_PART = [0, 1, 2, 0, 1, 0]
NS = D * len(Q_PART)
NM = NS + 3
PAIRS = NH // 2
UNITS = 3 * PAIRS
ALL_UNITS = B * UNITS
GROUP = UNITS // 2

MAX_UNITS = [(0, 0, 8, 128)] + [(1, 4 * i, 4, 256) for i in range(2)] \
    + [(2, 2 * i, 2, 384) for i in range(4)] + [(3, 2 * i, 2, 512) for i in range(4)]
NMAX = len(MAX_UNITS)


def side_jobs(b, u):
    jobs = {
        1: [("heads_out", b - 1, 1)],
        2: [("attn_turn", b - 1)],
        3: [("attn_proj", b - 1)],
        4: [("q", b + 2)],
        5: [("k", b + 2)],
        6: [("v", b + 2)],
        7: [("heads_out", b, 0)],
        8: [("freq", b - 1)],
        9: [("max_rows", b + 1)],
        10: [("freq_sum", b - 1)],
    }.get(u, [])
    return [j for j in jobs if 0 <= j[1] < B]


def max_units(b, u):
    if b + 1 >= B:
        return []
    return {0: [0], 1: [1], 2: [2], 3: [3, 4], 4: [5], 5: [6, 7], 6: [8], 7: [9], 8: [10]}.get(u, [])


START_JOBS = [("q", 0), ("k", 0), ("v", 0), ("q", 1), ("k", 1), ("v", 1), ("ctx_k",), ("ctx_vT",)] \
    + [("w_turn", i) for i in range(3)] \
    + [(n, b) for b in range(B) for n in ("ctx_kf", "ctx_z")] + [("ctx_vo",)]
TAIL_JOBS = [("heads_out", B - 1, 1), ("attn_turn", B - 1), ("attn_proj", B - 1), ("freq", B - 1),
             ("freq_sum", B - 1), ("inverse",)]
MISC = START_JOBS + [("max_rows", 0)] + [j for b in range(B) for u in range(UNITS) for j in side_jobs(b, u)] \
    + TAIL_JOBS
ORDER = {j: n for n, j in enumerate(MISC)}
NMISC = len(MISC)


def decoder_layer(nc, x_in, xT_in, wq_in, wk_in, wv_in, wp_in, bp_in, ctxT_in, cwq_in, cwqT_in, cbq_in, cwk_in, cbk_in,
                  cwv_in, cbv_in, cwo_in, cbo_in, wg_in, wu_in, wd_in, dft_in, idft_in, parts_in, out):
    with ExitStack() as ctx:
        def sb(name, shape, dt=F32):
            return ctx.enter_context(nc.sbuf_tensor(name, shape, dt))

        def sem(name):
            return ctx.enter_context(nc.semaphore(name))

        W = NI * B * T
        early_q, early_p, early_x = sb("early_q", [P, W]), sb("early_p", [P, W]), sb("early_x", [P, W])
        early_w, early_z = sb("early_w", [P, 3 * 3 * NB * BLK]), sb("early_z", [P, B * T])
        bt = "p (b t) -> p b t"
        probs, xT = early_p[:, 0:8 * T].rearrange("p (i q) -> p i q", i=4), early_p[:, 8 * T:W].rearrange(bt, b=B)
        dft, idft = (early_x[:, i * B * T:(i + 1) * B * T].rearrange("p (n t) -> p n t", n=NT) for i in range(2))
        x = early_x[:, 2 * B * T:W].rearrange("p (b n c) -> p b n c", b=B, n=NT)
        qstack = [early_q[:, i * NH * T // 2:(i + 1) * NH * T // 2].bitcast(BF16).rearrange("p (h t) -> p h t", h=NH)
                  for i in range(3)]
        wdiv, wint, wdq = (early_w[:, i * 3 * NB * BLK:(i + 1) * 3 * NB * BLK]
                           .rearrange("p (w k e) -> p w k e", w=3, k=NB) for i in range(3))
        zT = early_z[:, :].rearrange(bt, b=B)
        gate, up = early_q[:, :].rearrange(bt, b=B), early_p[:, :].rearrange(bt, b=B)
        gate16, sig16 = (early_x[:, i * W // 2:(i + 1) * W // 2].bitcast(d).rearrange(bt, b=B)
                         for i, d in enumerate((I16, U16)))
        up16 = early_w[:, 0:W // 2].bitcast(I16).rearrange(bt, b=B)
        xq = early_z[:, :].rearrange(bt, b=B)
        wq, wk6, wv, wp = sb("wq", [P, NH * D]), sb("wk6", [P, len(Q_PART), D]), sb("wv", [P, D]), sb("wp", [P, C])
        bp, bo, bk = sb("bp", [P, C]), sb("bo", [P, C]), sb("bk", [P, C])
        parts = sb("parts", [NS, 2])
        ident, identb = sb("ident", [P, P]), sb("identb", [P, P], BF16)
        maskf, maskb = sb("maskf", [P, P]), sb("maskb", [P, P], BF16)
        ones = sb("ones", [P, P])
        qpart = [[sb(f"q{n}_{i}", [P, T], BF16) for n in range(3)] for i in range(2)]
        qrest = sb("qrest", [P, T])
        kstack = [sb(f"kstack{i}", [P, T], BF16) for i in range(3)]
        kfirst, krest = sb("kfirst", [NS, T], BF16), sb("krest", [NS, T])
        ksecond, kdrop = sb("ksecond", [NS, T], BF16), sb("kdrop", [NS, T])
        vaug = [sb(f"vaug{i}", [P, NT, 32]) for i in range(3)]
        mneg = sb("mneg", [P, NT, NH])
        mrest = sb("mrest", [P, NT, NH])
        mparts = sb("mparts", [P, NT, 3, NH], BF16)
        mrow = sb("mrow", [3 * NH, T], BF16)
        headsT = [sb(f"headsT{g}", [P, T]) for g in range(2)]
        sumr = sb("sumr", [P, NT * 4])
        attn = sb("attn", [P, NT, 2, 4, D])
        attnT = sb("attnT", [P, T])
        z = sb("z", [P, NT, C])
        stats, mv = sb("stats", [P, NT, 6]), sb("mv", [P, NT, 2])
        veps, rstd, half = sb("veps", [P, NT]), sb("rstd", [P, NT]), sb("half", [P, NT])
        x1 = sb("x1", [P, B, NT, C])
        x1b = sb("x1b", [P, B, NT, C])
        ctxT = sb("ctxT", [P, B, S2])
        cwq, cwqT, cwk, cwv, cwo = (sb(n, [P, C]) for n in ("cwq", "cwqT", "cwk", "cwv", "cwo"))
        bq, bv = sb("bq", [P, 1]), sb("bv", [P, 1])
        bqT = sb("bqT", [P, 1])
        ctxk = sb("ctxk", [S2, B, C])
        kfT = sb("kfT", [P, T])
        kf0 = sb("kf0", [P, B, P])
        vT = sb("vT", [P, B, S2])
        vo = sb("vo", [S2, B, C])
        prod = sb("prod", [P, T])
        spec = sb("spec", [P, NT, B])
        corr, corr2, corr3, ecorr = (sb(n, [B, T]) for n in ("corr", "corr2", "corr3", "ecorr"))
        top1, top2, sel = sb("top1", [B, 8]), sb("top2", [B, 8]), sb("sel", [B, 8])
        ntop, wsum, wrec = sb("ntop", [B, 1]), sb("wsum", [B, 1]), sb("wrec", [B, 1])
        wts = sb("wts", [B, T])
        wrap = sb("wrap", [B, T + P])
        shift = [sb(f"shift{b}", [S2, T]) for b in range(B)]
        wraw = sb("wraw", [P, 3, NB, BLK])
        wmax, wscl, winv = (sb(n, [P, 3, NB]) for n in ("wmax", "wscl", "winv"))
        wT = sb("wT", [P, 3, NI, P])
        x2 = sb("x2", [P, B, NT, C])
        xround = sb("xround", [P, B, T])
        amax = sb("amax", [P, 4, 16])
        amax1 = sb("amax1", [P, 4])
        grow = sb("grow", [1, 4])
        scl = sb("scl", [P, 32])
        y3 = xround[:, :, :].rearrange("p b (n c) -> p b n c", n=NT)

        ps = ctx.enter_context(nc.psum_tensor("ps", [P, 8, T], F32))
        scoreT = [ps[:, 2 * i:2 * i + 2, :] for i in range(2)]
        smax = ps[:, 4:6, :]
        heads = ps[:, 6, :]
        misc = ps[:, 7, :]

        qdram = nc.dram_tensor("q_parts", [B, 3, P, T], BF16, kind="Internal").ap()

        s_x = [sem(f"x_landed{b}") for b in range(B)]
        s_xn = sem("x_nat_landed")
        s_wqkv = sem("wqkv_landed")
        s_wp = sem("wp_landed")
        s_cw = sem("ctx_weights_landed")
        s_dft, s_idft = sem("dft_landed"), sem("idft_landed")
        s_wf = sem("ffn_weights_landed")
        s_const = sem("consts_made")
        s_ident = sem("ident_made")
        misc_filled, misc_free = sem("misc_filled"), sem("misc_free")
        q1_made, q_rest, q23_made = sem("q1_made"), sem("q_rest"), sem("q23_made")
        q_in_dram, q_landed = sem("q_in_dram"), [sem(f"q_landed{i}") for i in range(3)]
        k1_made, k_rest, k_made = sem("k1_made"), sem("k_rest"), sem("k_made")
        v_made = sem("v_made")
        smax_filled, smax_read = sem("smax_filled"), sem("smax_read")
        mparts_made, mrow_made = sem("mparts_made"), sem("mrow_made")
        m_landed = sem("m_landed")
        scores_filled, exp_done, probs_ready, pv_done = (sem(n) for n in ("scores_filled", "exp_done", "probs_ready", "pv_done"))
        heads_read = sem("heads_read")
        attn_made, attnT_made = sem("attn_made"), sem("attnT_made")
        var_made, rstd_made, x1_made, x1b_made = sem("var_made"), sem("rstd_made"), sem("x1_made"), sem("x1b_made")
        xb_made = sem("xb_made")
        ctx_made = sem("ctx_made")
        kf_made = sem("kf_made")
        z_made = sem("z_made")
        w_made, wT_made = sem("w_made"), sem("wT_made")
        prod_made, spec_made = sem("prod_made"), sem("spec_made")
        top_made, ecorr_made = sem("top_made"), sem("ecorr_made")
        wrap_made = sem("wrap_made")
        shift_landed = [sem(f"shift_landed{b}") for b in range(B)]
        agg_filled, agg_read = sem("agg_filled"), sem("agg_read")
        x2_made, x2T_filled, x2T_read, xq_made = sem("x2_made"), sem("x2T_filled"), sem("x2T_read"), sem("xq_made")
        max_col, max_rowed, max_one, max_all = sem("max_col"), sem("max_rowed"), sem("max_one"), sem("max_all")
        h_filled, h_out = sem("h_filled"), sem("h_out")
        g16_made, sig_made, u16_made = sem("g16_made"), sem("sig_made"), sem("u16_made")
        scales_u = sem("scales_u")
        oround_made, oq_made, down_filled, down_read = sem("oround_made"), sem("oq_made"), sem("down_filled"), sem("down_read")
        y_made, y_stored = sem("y_made"), sem("y_stored")
        pool_ch, dve_ch = sem("pool_chain"), sem("dve_chain")

        block = ctx.enter_context(nc.Block())

        SX, FX, SG, FG, SU, FU, CH, SH, FH, CO, SO, FO, TMP = range(13)

        def col(n):
            return scl[:, n:n + 1]

        def shifted(b):
            a = wrap[b:b + 1, P:P + 1]
            return bass.AP(tensor=a.tensor, offset=a.offset, ap=[a.ap[0], [-1, S2], [1, T]])

        def landed(eng, job):
            eng.wait_ge(misc_filled, ORDER[job] + 1)

        @block.sync
        def _(sp):
            sp.dma_start(xT[:, 0, :], xT_in[:, 0:T]).then_inc(s_x[0], 16)
            sp.dma_start(wq[:, :], wq_in).then_inc(s_wqkv, 16)
            sp.dma_start(wk6[:, :, :], bass.AP(tensor=wk_in.tensor, offset=wk_in.offset,
                                               ap=[[D, P], [0, len(Q_PART)], [1, D]])).then_inc(s_wqkv, 16)
            sp.dma_start(wv[:, :], wv_in).then_inc(s_wqkv, 16)
            sp.dma_start(parts[:, :], parts_in).then_inc(s_wqkv, 16)
            sp.dma_start(xT[:, 1, :], xT_in[:, T:2 * T]).then_inc(s_x[1], 16)

            def bounce(b):
                for n in range(3):
                    if n == 0:
                        sp.wait_ge(q1_made, b + 1)
                    else:
                        sp.wait_ge(q23_made, 2 * b + n)
                    sp.dma_start(qdram[b, n], qpart[b % 2][n][:, :]).then_inc(q_in_dram, 16)
                sp.wait_ge(q_in_dram, 48 * (b + 1))
                if b >= 3:
                    sp.wait_ge(pv_done, UNITS * (b - 2))
                for r, n in enumerate(Q_PART):
                    sp.dma_start(qstack[b % 3][r * D:(r + 1) * D, :, :],
                                 qdram[b, n].rearrange("(h d) q -> d h q", d=D)).then_inc(q_landed[b % 3], 16)

            def max_rows(b):
                sp.wait_ge(mrow_made, b + 1)
                for n in range(3):
                    sp.dma_start(qstack[b % 3][NS + n:NS + n + 1, :, :],
                                 mrow[n * NH:(n + 1) * NH, :]).then_inc(m_landed, 16)

            bounce(0)
            bounce(1)
            for b in range(2, B):
                sp.dma_start(xT[:, b, :], xT_in[:, b * T:(b + 1) * T]).then_inc(s_x[b], 16)
            sp.dma_start(idft[:, :, :], idft_in.rearrange("(n p) l -> p n l", p=P)).then_inc(s_idft, 16)
            max_rows(0)
            for b in range(B):
                if b + 2 < B:
                    bounce(b + 2)
                if b + 1 < B:
                    max_rows(b + 1)
            sp.wait_ge(wrap_made, 1)
            for b in range(0, B, 2):
                sp.dma_start(shift[b][:, :], shifted(b)).then_inc(shift_landed[b], 16)
            for b in range(B):
                sp.wait_ge(y_made, b + 1)
                sp.dma_start(out[b].rearrange("(n p) c -> p n c", p=P), y3[:, b]).then_inc(y_stored, 16)
            sp.wait_ge(y_stored, 16 * B)

        @block.gpsimd
        def _(pool):
            chain = [0]

            def link(ins):
                chain[0] += 1
                ins.then_inc(pool_ch, 1)
                pool.wait_ge(pool_ch, chain[0])

            g = nc.gpsimd
            g.memset(ones[:, :], 1.0)
            link(g.memset(ident[:, :], 0.0))
            g.affine_select(out=ident[:, :], in_=ident[:, :], compare_op=ALU.not_equal, fill=1.0, base=0,
                            pattern=[[-1, P]], channel_multiplier=1).then_inc(s_ident, 1)
            link(g.memset(maskf[:, :], 0.0))
            link(g.affine_select(out=maskf[:, :], in_=maskf[:, :], compare_op=ALU.is_ge, fill=LOWEST, base=0,
                                 pattern=[[-1, P]], channel_multiplier=1))
            g.tensor_copy(maskb[:, :], maskf[:, :])
            pool.wait_ge(s_ident, 1)
            for i in range(3):
                link(g.memset(vaug[i][:, :, :], 0.0))
                g.memset(vaug[i][:, :, D:D + 1], 1.0)
            g.memset(half[:, :], -0.5)
            g.tensor_copy(identb[:, :], ident[:, :]).then_inc(s_const, 1)

            def q_parts(b):
                pool.wait_ge(q_rest, b + 1)
                if b >= 2:
                    pool.wait_ge(q_in_dram, 48 * (b - 1))
                ins = g.tensor_copy(qpart[b % 2][1][:, :], qrest[:, :]).then_inc(q23_made, 1)
                pool.wait_ge(q23_made, 2 * b + 1)
                g.tensor_tensor(qpart[b % 2][2][:, :], qrest[:, :], qpart[b % 2][1][:, :], ALU.subtract)\
                    .then_inc(q23_made, 1)

            def k_parts(b):
                pool.wait_ge(k_rest, b + 1)
                if b >= 3:
                    pool.wait_ge(pv_done, UNITS * (b - 2))
                link(g.tensor_copy(ksecond[:, :], krest[:, :]))
                link(g.tensor_scalar(kdrop[:, :], ksecond[:, :], parts[:, 1:2], None, ALU.mult))
                g.tensor_tensor(kstack[b % 3][0:NS, :], kdrop[:, :], krest[:, :], ALU.subtract).then_inc(k_made, 1)

            def inv_std(n):
                pool.wait_ge(var_made, n + 1)
                link(g.tensor_scalar(veps[:, :], mv[:, :, 1], EPS, None, ALU.add))
                g.tensor_tensor(rstd[:, :], veps[:, :], half[:, :], ALU.pow).then_inc(rstd_made, 1)

            def add_bo(b):
                pool.wait_ge(x1_made, b + 1)
                g.tensor_tensor(x1b[:, b], x1[:, b], bo[:, None, :].to_broadcast([P, NT, C]) if False else bo_b, ALU.add)\
                    .then_inc(x1b_made, 1)

            bo_b = bass.AP(tensor=bo[:, :].tensor, offset=bo[:, :].offset, ap=[bo[:, :].ap[0], [0, NT], [1, C]])
            bp_b = bass.AP(tensor=bp[:, :].tensor, offset=bp[:, :].offset, ap=[bp[:, :].ap[0], [0, NT], [1, C]])

            def select(n):
                u = n % UNITS
                pool.wait_ge(exp_done, n + 1)
                pt = probs[:, n % 4, :]
                kinds = [(0, T)] if u % 3 == 0 else [(0, T - P)] if u % 3 == 1 else [(0, 2 * P), (T, P)]
                for off, w in kinds:
                    v = pt[:, off:off + 2 * w].rearrange("p (h q) -> p h q", h=2)[:, :, 0:P]
                    last = g.affine_select(out=v, in_=v, compare_op=ALU.is_ge, fill=0.0, base=0,
                                           pattern=[[0, 2], [1, P]], channel_multiplier=-1)
                last.then_inc(probs_ready, 1)

            pool.wait_ge(s_wqkv, 64)
            q_parts(0)
            k_parts(0)
            q_parts(1)
            k_parts(1)
            pool.wait_ge(s_cw, 160)
            g.tensor_scalar(bqT[:, :], bq[:, :], float(T), None, ALU.mult).then_inc(ctx_made, 1)
            pool.wait_ge(s_wp, 32)
            pool.wait_ge(s_xn, 16)
            for b in range(B):
                g.tensor_tensor(x[:, b], x[:, b], bp_b, ALU.add).then_inc(xb_made, 1)
            select(0)
            for b in range(B):
                for u in range(UNITS):
                    if b * UNITS + u + 1 < ALL_UNITS:
                        select(b * UNITS + u + 1)
                    for job in side_jobs(b, u):
                        if job[0] == "q":
                            q_parts(job[1])
                        if job[0] == "k":
                            k_parts(job[1])
                        if job[0] == "attn_proj":
                            inv_std(job[1])
                    if b >= 1 and u == 6:
                        add_bo(b - 1)
            inv_std(B - 1)
            add_bo(B - 1)
            for n in range(B, 3 * B):
                inv_std(n)

        @block.scalar
        def _(act):
            s = nc.scalar
            act.dma_start(x[:, :, :, :], x_in.rearrange("b (n p) c -> p b n c", p=P)).then_inc(s_xn, 16)
            act.dma_start(ctxT[:, :, :], ctxT_in).then_inc(s_cw, 16)
            for dst, src in ((cwk, cwk_in), (cwv, cwv_in), (cwqT, cwqT_in), (cwq, cwq_in), (cwo, cwo_in)):
                act.dma_start(dst[:, :], src).then_inc(s_cw, 16)
            for dst, src in ((bq, cbq_in), (bv, cbv_in)):
                act.dma_start(dst[:, :], src.rearrange("(c a) -> c a", a=1)).then_inc(s_cw, 16)
            for dst, src, sm in ((bk, cbk_in, s_cw), (bo, cbo_in, s_cw), (bp, bp_in, s_wp)):
                act.dma_start(dst[:, :], bass.AP(tensor=src.tensor, offset=src.offset, ap=[[0, P], [1, C]])).then_inc(sm, 16)
            act.dma_start(wp[:, :], wp_in).then_inc(s_wp, 16)
            act.dma_start(dft[:, :, :], dft_in.rearrange("(n p) f -> p n f", p=P)).then_inc(s_dft, 16)
            for n, w in enumerate((wg_in, wu_in)):
                act.dma_start(wraw[:, n].rearrange("p (i k) e -> p i (k e)", i=NI),
                              w.rearrange("(i p) c -> p i c", p=P)).then_inc(s_wf, 16)
            act.dma_start(wraw[:, 2].rearrange("p k e -> p (k e)"), wd_in).then_inc(s_wf, 16)

            def q_first(b):
                if b >= 2:
                    act.wait_ge(q_in_dram, 48 * (b - 1))
                landed(act, ("q", b))
                s.activation(qpart[b % 2][0][:, :], misc, ACT.Copy).then_inc(q1_made, 1)

            def k_first(b):
                if b >= 1:
                    act.wait_ge(k_rest, b)
                landed(act, ("k", b))
                s.activation(kfirst[:, :], misc[0:NS, :], ACT.Copy).then_inc(k1_made, 1)

            def v_out(b):
                landed(act, ("v", b))
                if b >= 3:
                    act.wait_ge(pv_done, UNITS * (b - 2))
                s.activation(vaug[b % 3][:, :, 0:D], misc[:, 0:NT * D].rearrange("p (n d) -> p n d", n=NT),
                             ACT.Copy).then_inc(misc_free, 1)

            def max_rows_out(b):
                landed(act, ("max_rows", b))
                if b >= 1:
                    act.wait_ge(m_landed, 48 * b)
                s.activation(mrow[:, :], misc[0:3 * NH, :], ACT.Copy).then_inc(mrow_made, 1)
                act.wait_ge(mrow_made, b + 1)
                act.sem_inc(misc_free, 1) if False else None

            def exps(n):
                u = n % UNITS
                act.wait_ge(scores_filled, n + 1)
                if n >= 4:
                    act.wait_ge(pv_done, n - 3)
                pt, sc = probs[:, n % 4, :], scoreT[n % 2]
                if u % 3 < 2:
                    w = T - P * (u % 3)
                    s.activation(pt[:, 0:2 * w].rearrange("p (h q) -> p h q", h=2), sc[:, :, 0:w],
                                 ACT.Exp, scale=SCALE).then_inc(exp_done, 1)
                else:
                    s.activation(pt[:, 0:T], sc[:, 0, :], ACT.Exp, scale=SCALE)
                    s.activation(pt[:, T:T + 2 * P], sc[:, 1, 0:2 * P], ACT.Exp, scale=SCALE).then_inc(exp_done, 1)

            def heads_evict(n):
                k = n // GROUP
                act.wait_ge(pv_done, n + 1)
                if k >= 2:
                    act.wait_ge(misc_filled, ORDER[("heads_out", k // 2 - 1, k % 2)] + 1)
                s.activation(headsT[k % 2][:, :], heads, ACT.Copy).then_inc(heads_read, 1)

            def side(job):
                kind = job[0]
                if kind == "q":
                    q_first(job[1])
                elif kind == "k":
                    k_first(job[1])
                elif kind == "v":
                    v_out(job[1])
                elif kind == "max_rows":
                    b = job[1]
                    landed(act, job)
                    if b >= 1:
                        act.wait_ge(m_landed, 48 * b)
                    s.activation(mrow[:, :], misc[0:3 * NH, :], ACT.Copy).then_inc(mrow_made, 1)
                elif kind == "attn_turn":
                    landed(act, job)
                    if job[1] >= 1:
                        act.wait_ge(misc_filled, ORDER[("attn_proj", job[1] - 1)] + 1)
                    s.activation(attnT[:, :], misc, ACT.Copy).then_inc(misc_free, 1)
                elif kind == "freq_sum":
                    landed(act, job)
                    s.activation(spec[:, :, job[1]], misc[:, 0:NT], ACT.Copy).then_inc(misc_free, 1)
                elif kind == "ctx_vT":
                    landed(act, job)
                    s.activation(vT[:, :, :], misc[:, 0:B * S2].rearrange("p (b s) -> p b s", b=B), ACT.Identity,
                                 bias=bv[:, 0:1]).then_inc(misc_free, 1)
                elif kind == "w_turn":
                    landed(act, job)
                    s.activation(wT[:, job[1]], misc[:, 0:NI * P].rearrange("p (i o) -> p i o", i=NI), ACT.Copy)\
                        .then_inc(misc_free, 1)
                elif kind == "ctx_kf":
                    landed(act, job)
                    if job[1] >= 1:
                        act.wait_ge(misc_filled, ORDER[("ctx_z", job[1] - 1)] + 1)
                    s.activation(kfT[:, :], misc, ACT.Copy).then_inc(kf_made, 1)
                    s.activation(kf0[:, job[1], 0:1], misc[:, 0:1], ACT.Copy).then_inc(misc_free, 1)
                elif kind == "ctx_z":
                    landed(act, job)
                    s.activation(zT[:, job[1], :], misc, ACT.Copy).then_inc(misc_free, 1)
                elif kind == "ctx_vo":
                    landed(act, job)
                    s.activation(vo[:, :, :], misc[0:S2, :].rearrange("p (b c) -> p b c", b=B), ACT.Copy)\
                        .then_inc(misc_free, 1)

            act.wait_ge(s_const, 2)
            act.wait_ge(s_cw, 160)
            for job in START_JOBS:
                side(job)
            side(("max_rows", 0))
            exps(0)
            for b in range(B):
                for u in range(UNITS):
                    n = b * UNITS + u
                    if n + 1 < ALL_UNITS:
                        exps(n + 1)
                    for job in side_jobs(b, u):
                        side(job)
                    if u % GROUP == GROUP - 1:
                        heads_evict(n)
            for job in TAIL_JOBS:
                side(job)
            act.wait_ge(top_made, 1)
            s.activation(ecorr[:, :], corr[:, :], ACT.Exp, bias=ntop[:, 0:1]).then_inc(ecorr_made, 1)
            act.wait_ge(wrap_made, 1)
            for b in range(1, B, 2):
                act.dma_start(shift[b][:, :], shifted(b)).then_inc(shift_landed[b], 16)
            for b in range(B):
                act.wait_ge(x2T_read, b + 1)
                s.activation(xq[:, b], xround[:, b], ACT.Copy, bias=-MAGIC).then_inc(xq_made, 1)
            for k in range(2 * B * NI):
                hid = gate if k < B * NI else up
                kk = k % (B * NI)
                act.wait_ge(h_filled, k + 1)
                s.activation(hid[:, kk // NI, (kk % NI) * T:(kk % NI + 1) * T], ps[:, k % 6, :], ACT.Copy).then_inc(h_out, 1)
                if k >= B * NI and kk % NI == NI - 1:
                    b = kk // NI
                    act.wait_ge(g16_made, b + 1)
                    s.activation(gate[:, b], gate16[:, b], ACT.Sigmoid, scale=col(SG)).then_inc(sig_made, 1)
            act.wait_ge(scales_u, 1)
            for b in range(B):
                s.activation(up16[:, b], up[:, b], ACT.Copy, scale=col(FU)).then_inc(u16_made, 1)
            for b in range(B):
                act.wait_ge(oround_made, b + 1)
                s.activation(up[:, b], gate[:, b], ACT.Copy, bias=-MAGIC).then_inc(oq_made, 1)

        @block.vector
        def _(dve):
            v = nc.vector
            chain = [0]

            def link(ins):
                chain[0] += 1
                ins.then_inc(dve_ch, 1)
                dve.wait_ge(dve_ch, chain[0])

            def max_unit(b, i):
                t, h, n, w = MAX_UNITS[i]
                dve.wait_ge(smax_filled, NMAX * b + i + 1)
                if n * w == 2 * T:
                    src = smax.rearrange("p k c -> p (k c)").rearrange("p (h s) -> p h s", h=n)
                else:
                    src = smax[:, :, 0:w]
                v.tensor_reduce(mneg[:, t, h:h + n], src, AX.X, ALU.max, negate=True).then_inc(smax_read, 1)
                if i == NMAX - 1:
                    if b >= 1:
                        dve.wait_ge(misc_filled, ORDER[("max_rows", b - 1)] + 1)
                    dve.wait_ge(smax_read, NMAX * (b + 1))
                    link(v.tensor_copy(mparts[:, :, 0, :], mneg[:, :, :]))
                    link(v.tensor_tensor(mrest[:, :, :], mneg[:, :, :], mparts[:, :, 0, :], ALU.subtract))
                    link(v.tensor_copy(mparts[:, :, 1, :], mrest[:, :, :]))
                    v.tensor_tensor(mparts[:, :, 2, :], mrest[:, :, :], mparts[:, :, 1, :], ALU.subtract)\
                        .then_inc(mparts_made, 1)

            def norm_stats(n):
                for t in range(NT):
                    ins = v.bn_stats(stats[:, t, :], z[:, t, :])
                link(ins)
                for t in range(NT):
                    ins = v.bn_aggr(mv[:, t, :], stats[:, t, :])
                ins.then_inc(var_made, 1)

            def normalise(n, dst):
                dve.wait_ge(rstd_made, n + 1)
                dve.wait_ge(var_made, n + 1)
                for t in range(NT):
                    ins = v.tensor_scalar(dst[:, t, :], z[:, t, :], mv[:, t, 0:1], rstd[:, t:t + 1],
                                          ALU.subtract, ALU.mult)
                return ins

            bk_b = bass.AP(tensor=bk[:, :].tensor, offset=bk[0:S2, :].offset, ap=[bk[0:S2, :].ap[0], [0, B], [1, C]])

            def side(job):
                kind = job[0]
                if kind == "q":
                    b = job[1]
                    if b >= 1:
                        dve.wait_ge(q23_made, 2 * b)
                    dve.wait_ge(q1_made, b + 1)
                    v.tensor_tensor(qrest[:, :], misc, qpart[b % 2][0][:, :], ALU.subtract).then_inc(q_rest, 1)
                elif kind == "k":
                    b = job[1]
                    if b >= 1:
                        dve.wait_ge(k_made, b)
                    dve.wait_ge(k1_made, b + 1)
                    v.scalar_tensor_tensor(krest[:, :], kfirst[:, :], parts[:, 0:1], misc[0:NS, :],
                                           ALU.mult, ALU.subtract).then_inc(k_rest, 1)
                elif kind == "heads_out":
                    _, b, g = job
                    landed(dve, job)
                    if g == 0 and b >= 1:
                        dve.wait_ge(misc_filled, ORDER[("attn_turn", b - 1)] + 1)
                    src = misc.rearrange("p (k e) -> p k e", e=32)
                    link(v.reciprocal(sumr[:, :], src[:, :, D]))
                    rec = sumr[:, :]
                    rec = bass.AP(tensor=rec.tensor, offset=rec.offset, ap=[rec.ap[0], [4, NT], [1, 4], [0, D]])
                    v.tensor_tensor(attn[:, :, g], misc.rearrange("p (t h e) -> p t h e", t=NT, h=4)[:, :, :, 0:D], rec,
                                    ALU.mult).then_inc(misc_free, 1)
                elif kind == "attn_proj":
                    b = job[1]
                    landed(dve, job)
                    dve.wait_ge(xb_made, b + 1)
                    dve.wait_ge(x1_made, b)
                    ins = v.tensor_tensor(z[:, :, :], misc.rearrange("p (t c) -> p t c", t=NT), x[:, b], ALU.add)
                    ins.then_inc(misc_free, 1)
                    dve.wait_ge(misc_free, FREED[ORDER[job] + 1])
                    norm_stats(b)
                elif kind == "freq":
                    b = job[1]
                    landed(dve, job)
                    v.tensor_tensor(prod[:, :], misc, zT[:, b, :], ALU.mult).then_inc(misc_free, 1)
                elif kind == "ctx_k":
                    landed(dve, job)
                    v.tensor_tensor(ctxk[:, :, :], misc[0:S2, :].rearrange("p (b c) -> p b c", b=B), bk_b, ALU.add)\
                        .then_inc(misc_free, 1)

            for i in range(3):
                v.memset(kstack[i][NS:NS + 32, :], 1.0)
            ins = v.memset(kf0[:, :, :], 0.0)
            ins.then_inc(s_const, 1)
            dve.wait_ge(s_wqkv, 64)
            dve.wait_ge(s_cw, 160)
            for job in START_JOBS[:START_JOBS.index(("ctx_k",)) + 1]:
                side(job)
            dve.wait_ge(s_wf, 48)
            w3 = wraw[:, :, :, :].rearrange("p w k e -> p (w k) e")
            link(v.tensor_reduce(wmax[:, :, :].rearrange("p w k -> p (w k)"), w3, AX.X, ALU.max, apply_absolute_value=True))
            link(v.tensor_scalar(wscl[:, :, :], wmax[:, :, :], 1.0 / 7.0, 1e-12, ALU.mult, ALU.max))
            link(v.reciprocal(winv[:, :, :], wscl[:, :, :]))
            sw, iw = (bass.AP(tensor=a.tensor, offset=a.offset, ap=[a.ap[0], [1, 3 * NB], [0, BLK]])
                      for a in (wscl[:, :, :], winv[:, :, :]))
            flat = "p w k e -> p (w k) e"
            link(v.tensor_tensor(wdiv[:, :, :, :].rearrange(flat), w3, iw, ALU.mult))
            link(v.tensor_scalar(wint[:, :, :, :], wdiv[:, :, :, :], MAGIC, MAGIC, ALU.add, ALU.subtract))
            link(v.tensor_scalar(wdiv[:, :, :, :], wint[:, :, :, :], -8.0, 7.0, ALU.max, ALU.min))
            v.tensor_tensor(wdq[:, :, :, :].rearrange(flat), wdiv[:, :, :, :].rearrange(flat), sw, ALU.mult)\
                .then_inc(w_made, 1)
            for i in range(NMAX):
                max_unit(0, i)
            for b in range(B):
                for u in range(UNITS):
                    for job in side_jobs(b, u):
                        side(job)
                    for i in max_units(b, u):
                        max_unit(b + 1, i)
                    if b >= 1 and u == 5:
                        normalise(b - 1, x1[:, b - 1]).then_inc(x1_made, 1)
            for job in TAIL_JOBS[:3]:
                side(job)
            normalise(B - 1, x1[:, B - 1]).then_inc(x1_made, 1)
            side(TAIL_JOBS[3])
            landed(dve, ("inverse",))
            link(v.tensor_copy(corr[:, :], misc[0:B, :]))
            link(v.max(top1[:, :], corr[:, :]))
            v.tensor_scalar(ntop[:, :], top1[:, 0:1], -1.0, None, ALU.mult).then_inc(top_made, 1)
            link(v.match_replace(corr2[:, :], top1[:, :], corr[:, :], LOWEST))
            link(v.max(top2[:, :], corr2[:, :]))
            v.tensor_copy(sel[:, 0:TOPK - 8], top2[:, 0:TOPK - 8])
            link(v.memset(sel[:, TOPK - 8:8], LOWEST))
            link(v.match_replace(corr3[:, :], sel[:, :], corr2[:, :], LOWEST))
            dve.wait_ge(ecorr_made, 1)
            link(v.scalar_tensor_tensor(wts[:, :], corr3[:, :], LOWEST, ecorr[:, :], ALU.is_equal, ALU.mult,
                                        accum_out=wsum[:, :]))
            link(v.reciprocal(wrec[:, :], wsum[:, :]))
            a = wts[:, :]
            back = bass.AP(tensor=a.tensor, offset=a.offset + T - 1, ap=[a.ap[0], [-1, T - 1]])
            v.tensor_scalar(wrap[:, P + 1:P + T], back, wrec[:, 0:1], None, ALU.mult)
            v.tensor_scalar(wrap[:, P:P + 1], wts[:, 0:1], wrec[:, 0:1], None, ALU.mult)
            back = bass.AP(tensor=a.tensor, offset=a.offset + P, ap=[a.ap[0], [-1, P]])
            v.tensor_scalar(wrap[:, 0:P], back, wrec[:, 0:1], None, ALU.mult).then_inc(wrap_made, 1)

            for b in range(B):
                n = B + b
                dve.wait_ge(agg_filled, b + 1)
                dve.wait_ge(x1b_made, b + 1)
                dve.wait_ge(x1_made, B)
                if b >= 1:
                    dve.wait_ge(x2_made, b)
                v.tensor_tensor(z[:, :, :], ps[:, b, :].rearrange("p (t c) -> p t c", t=NT), x1b[:, b], ALU.add)\
                    .then_inc(agg_read, 1)
                dve.wait_ge(agg_read, b + 1)
                norm_stats(n)
                normalise(n, x2[:, b]).then_inc(x2_made, 1)
                dve.wait_ge(x2_made, b + 1)
                last = v.tensor_reduce(amax[:, 0, b:b + 1], x2[:, b].rearrange("p t c -> p (t c)"), AX.X, ALU.max,
                                       apply_absolute_value=True)
            link(last)

            rounds = [0]

            def across(which, count, n):
                for i, k in enumerate(which):
                    ins = v.tensor_reduce(amax1[:, i:i + 1], amax[:, k, 0:count], AX.X, ALU.max)
                ins.then_inc(max_col, 1)
                dve.wait_ge(max_rowed, n + 1)
                v.tensor_reduce(grow[:, 0:len(which)],
                                misc[0:1, 0:len(which) * P].rearrange("p (w c) -> p w c", c=P), AX.X, ALU.max)\
                    .then_inc(max_one, 1)
                dve.wait_ge(max_all, n + 1)

            def scale_of(m, c, s_out, f_out):
                if c is None:
                    link(v.tensor_scalar(col(s_out), m, 1.0 / QMAX, 1e-12, ALU.mult, ALU.max))
                    link(v.reciprocal(col(f_out), col(s_out)))
                    return
                link(v.tensor_scalar(col(TMP), m, col(c), 1.0 / QMAX, ALU.mult, ALU.mult))
                link(v.tensor_scalar(col(s_out), col(TMP), 1e-12, None, ALU.max))
                link(v.reciprocal(col(TMP), col(s_out)))
                link(v.tensor_tensor(col(f_out), col(TMP), col(c), ALU.mult))

            across([0], B, 0)
            scale_of(misc[:, 0:1], None, SX, FX)
            for b in range(B):
                dve.wait_ge(x2T_filled, b + 1)
                v.tensor_scalar(xround[:, b], ps[:, [4, 5, 6, 0][b], :], col(FX), MAGIC, ALU.mult, ALU.add)\
                    .then_inc(x2T_read, 1)

            def hidden_max(hid, row, k):
                kk = k % (B * NI)
                dve.wait_ge(h_out, k + 1)
                return v.tensor_reduce(amax[:, row, kk:kk + 1], hid[:, kk // NI, (kk % NI) * T:(kk % NI + 1) * T], AX.X, ALU.max,
                                       apply_absolute_value=True)

            for k in range(B * NI):
                last = hidden_max(gate, 0, k)
            link(last)
            across([0], B * NI, 1)
            scale_of(misc[:, 0:1], SX, SG, FG)
            for b in range(B):
                v.tensor_scalar(gate16[:, b], gate[:, b], col(FG), None, ALU.mult).then_inc(g16_made, 1)
            link(v.tensor_scalar(col(CH), col(SG), 1.0 / 65536.0, None, ALU.mult))
            for b in range(B):
                for i in range(NI):
                    hidden_max(up, 1, (B + b) * NI + i)
                dve.wait_ge(sig_made, b + 1)
                link(v.tensor_scalar(sig16[:, b], gate[:, b], 65536.0, 65535.0, ALU.mult, ALU.min))
                link(v.tensor_tensor(gate[:, b], gate16[:, b], sig16[:, b], ALU.mult))
                last = v.tensor_reduce(amax[:, 2, b:b + 1], gate[:, b], AX.X, ALU.max, apply_absolute_value=True)
            link(last)
            link(v.tensor_reduce(amax[:, 3, 0:1], amax[:, 2, 0:B], AX.X, ALU.max))
            link(v.tensor_reduce(amax[:, 3, 1:2], amax[:, 1, 0:B * NI], AX.X, ALU.max))
            ins = v.tensor_copy(amax1[:, 0:2], amax[:, 3, 0:2])
            ins.then_inc(max_col, 1)
            dve.wait_ge(max_rowed, 3)
            v.tensor_reduce(grow[:, 0:2], misc[0:1, 0:2 * P].rearrange("p (w c) -> p w c", c=P), AX.X, ALU.max)\
                .then_inc(max_one, 1)
            dve.wait_ge(max_all, 3)
            scale_of(misc[:, 1:2], SX, SU, FU)
            v.tensor_copy(col(CO), col(SU)).then_inc(scales_u, 1)
            dve.wait_ge(scales_u, 1)
            scale_of(misc[:, 0:1], CH, SH, FH)
            link(v.tensor_tensor(col(CO), col(SH), col(SU), ALU.mult))
            for b in range(B):
                link(v.tensor_scalar(gate16[:, b], gate[:, b], col(FH), None, ALU.mult))
                dve.wait_ge(u16_made, b + 1)
                link(v.tensor_tensor(gate[:, b], gate16[:, b], up16[:, b], ALU.mult))
                last = v.tensor_reduce(amax[:, 0, b:b + 1], gate[:, b], AX.X, ALU.max, apply_absolute_value=True)
            link(last)
            across([0], B, 3)
            scale_of(misc[:, 0:1], CO, SO, FO)
            for b in range(B):
                v.tensor_scalar(gate[:, b], gate[:, b], col(FO), MAGIC, ALU.mult, ALU.add).then_inc(oround_made, 1)
            for b in range(B):
                n = 2 * B + b
                dve.wait_ge(down_filled, b + 1)
                if b >= 1:
                    dve.wait_ge(y_made, b)
                v.scalar_tensor_tensor(z[:, :, :].rearrange("p t c -> p (t c)"), ps[:, b, :], col(SO),
                                       x2[:, b].rearrange("p t c -> p (t c)"), ALU.mult, ALU.add).then_inc(down_read, 1)
                dve.wait_ge(down_read, b + 1)
                norm_stats(n)
                normalise(n, y3[:, b]).then_inc(y_made, 1)

        @block.tensor
        def _(pe):
            mm = nc.tensor.matmul

            def score_unit(n):
                b, u = divmod(n, UNITS)
                p, kind = divmod(u, 3)
                if n >= 2:
                    pe.wait_ge(exp_done, n - 1)
                if u == 0:
                    pe.wait_ge(m_landed, 48 * (b + 1))
                q, k, sc = qstack[b % 3], kstack[b % 3], scoreT[n % 2]
                for hh in range(2):
                    h = 2 * p + hh
                    if kind < 2:
                        last = mm(sc[:, hh, 0:T - P * kind], k[0:NM, P * kind:P * (kind + 1)], q[0:NM, h, P * kind:T],
                                  start=True, stop=True)
                    else:
                        for j in (2, 3):
                            w = T - P * j
                            last = mm(sc[:, j - 2, hh * w:(hh + 1) * w], k[0:NM, P * j:P * (j + 1)], q[0:NM, h, P * j:T],
                                      start=True, stop=True)
                last.then_inc(scores_filled, 1)

            def value_unit(n):
                b, u = divmod(n, UNITS)
                p, kind = divmod(u, 3)
                pe.wait_ge(probs_ready, n + 1)
                if u % GROUP == 0 and n > 0:
                    pe.wait_ge(heads_read, n // GROUP)
                pt, va = probs[:, n % 4, :], vaug[b % 3]
                for hh in range(2):
                    r = 32 * ((2 * p + hh) % 4)
                    if kind < 2:
                        w = T - P * kind
                        last = mm(heads[r:r + 32, P * kind:T], va[:, kind, :], pt[:, hh * w:(hh + 1) * w],
                                  start=(kind == 0), stop=False)
                    else:
                        mm(heads[r:r + 32, 2 * P:T], va[:, 2, :], pt[:, hh * 2 * P:(hh + 1) * 2 * P], start=False, stop=False)
                        last = mm(heads[r:r + 32, 3 * P:T], va[:, 3, :], pt[:, T + hh * P:T + (hh + 1) * P],
                                  start=False, stop=True)
                last.then_inc(pv_done, 1)

            def max_unit(b, i):
                t, h0, n, w = MAX_UNITS[i]
                if i == 0:
                    pe.wait_ge(q_landed[b % 3], 96 * (b // 3 + 1))
                    pe.wait_ge(k_made, b + 1)
                if NMAX * b + i >= 1:
                    pe.wait_ge(smax_read, NMAX * b + i)
                per = n // 2
                for h in range(n):
                    o = smax[:, h // per, (h % per) * w:(h % per + 1) * w]
                    mm(o, qstack[b % 3][0:NS, h0 + h, P * t:P * (t + 1)], kstack[b % 3][0:NS, 0:w], start=True, stop=False)
                    last = mm(o[:, w - P:w], identb[:, :], maskb[:, :], start=False, stop=True)
                last.then_inc(smax_filled, 1)

            def side(job):
                n, kind = ORDER[job], job[0]
                waits_for_bank(n)
                if kind == "q":
                    pe.wait_ge(s_x[job[1]], 16)
                    last = mm(misc, wq[:, :], xT[:, job[1], :], start=True, stop=True)
                elif kind == "k":
                    last = mm(misc[0:NS, :], wk6[:, :, :].rearrange("p r d -> p (r d)"), xT[:, job[1], :],
                              start=True, stop=True)
                elif kind == "v":
                    for t in range(NT):
                        last = mm(misc[:, t * D:(t + 1) * D], xT[:, job[1], P * t:P * (t + 1)], wv[:, :],
                                  start=True, stop=True)
                elif kind == "max_rows":
                    pe.wait_ge(mparts_made, job[1] + 1)
                    for t in range(NT):
                        last = mm(misc[0:3 * NH, P * t:P * (t + 1)], mparts[:, t].rearrange("p n h -> p (n h)"),
                                  identb[:, :], start=True, stop=True)
                elif kind == "heads_out":
                    _, b, g = job
                    pe.wait_ge(heads_read, 2 * b + g + 1)
                    for t in range(NT):
                        last = nc.tensor.transpose(misc[:, P * t:P * (t + 1)], headsT[g][:, P * t:P * (t + 1)], ident[:, :])
                elif kind == "attn_turn":
                    for t in range(NT):
                        last = nc.tensor.transpose(misc[:, P * t:P * (t + 1)], attn[:, t].rearrange("p g h d -> p (g h d)"),
                                                   ident[:, :])
                elif kind == "attn_proj":
                    for t in range(NT):
                        last = mm(misc[:, P * t:P * (t + 1)], attnT[:, P * t:P * (t + 1)], wp[:, :], start=True, stop=True)
                elif kind == "freq":
                    pe.wait_ge(x1_made, job[1] + 1)
                    for t in range(NT):
                        last = mm(misc, x1[:, job[1], t, :], dft[:, t, :], start=(t == 0), stop=(t == NT - 1))
                elif kind == "freq_sum":
                    for f in range(NT):
                        last = mm(misc[:, f:f + 1], prod[:, P * f:P * (f + 1)], ones[:, 0:1], start=True, stop=(f > 0))
                        if f == 0:
                            last = mm(misc[:, 0:1], kf0[:, job[1], :], bqT[:, :], start=False, stop=True)
                elif kind == "ctx_k":
                    pe.wait_ge(s_cw, 160)
                    pe.wait_ge(s_dft, 16)
                    for b in range(B):
                        last = mm(misc[0:S2, P * b:P * (b + 1)], ctxT[:, b, :], cwk[:, :], start=True, stop=True)
                elif kind == "ctx_vT":
                    last = mm(misc[:, 0:B * S2], cwv[:, :], ctxT[:, :, :].rearrange("p b s -> p (b s)"), start=True, stop=True)
                elif kind == "w_turn":
                    pe.wait_ge(w_made, 1)
                    for i in range(NI):
                        last = nc.tensor.transpose(misc[:, P * i:P * (i + 1)],
                                                   wdq[:, job[1]].rearrange("p k e -> p (k e)")[:, P * i:P * (i + 1)], ident[:, :])
                elif kind == "ctx_kf":
                    last = mm(misc, ctxk[:, job[1], :], dft[0:S2, 0, :], start=True, stop=True)
                elif kind == "ctx_z":
                    last = mm(misc, cwqT[:, :], kfT[:, :], start=True, stop=True)
                elif kind == "ctx_vo":
                    for b in range(B):
                        last = mm(misc[0:S2, P * b:P * (b + 1)], vT[:, b, :], cwo[:, :], start=True, stop=True)
                elif kind == "inverse":
                    pe.wait_ge(s_idft, 16)
                    for f in range(NT):
                        last = mm(misc[0:B, :], spec[:, f, :], idft[:, f, :], start=(f == 0), stop=(f == NT - 1))
                last.then_inc(misc_filled, 1)

            def waits_for_bank(n):
                if n == 0:
                    return
                before = MISC[n - 1]
                if before[0] == "q":
                    pe.wait_ge(q_rest, before[1] + 1)
                elif before[0] == "k":
                    pe.wait_ge(k_rest, before[1] + 1)
                elif before[0] == "max_rows":
                    pe.wait_ge(mrow_made, before[1] + 1)
                else:
                    pe.wait_ge(misc_free, FREED[n])

            pe.wait_ge(s_wqkv, 64)
            pe.wait_ge(s_const, 2)
            for job in START_JOBS:
                side(job)
            for i in range(NMAX):
                max_unit(0, i)
            side(("max_rows", 0))
            score_unit(0)
            for b in range(B):
                for u in range(UNITS):
                    n = b * UNITS + u
                    if n + 1 < ALL_UNITS:
                        score_unit(n + 1)
                    for job in side_jobs(b, u):
                        side(job)
                    for i in max_units(b, u):
                        max_unit(b + 1, i)
                    value_unit(n)
            for job in TAIL_JOBS:
                side(job)
            for b in range(B):
                pe.wait_ge(shift_landed[b], 16)
                for t in range(NT):
                    last = mm(ps[:, b, P * t:P * (t + 1)], shift[b][:, P * t:P * (t + 1)], vo[:, b, :],
                              start=True, stop=True)
                last.then_inc(agg_filled, 1)
            for b in range(B):
                pe.wait_ge(x2_made, b + 1)
                for t in range(NT):
                    last = nc.tensor.transpose(ps[:, [4, 5, 6, 0][b], P * t:P * (t + 1)], x2[:, b, t, :], ident[:, :])
                last.then_inc(x2T_filled, 1)

            def across(n, k):
                pe.wait_ge(max_col, n + 1)
                for i in range(k):
                    last = mm(misc[0:1, P * i:P * (i + 1)], amax1[:, i:i + 1], ident[:, :], start=True, stop=True)
                last.then_inc(max_rowed, 1)

            def back(n, k):
                pe.wait_ge(max_one, n + 1)
                mm(misc[:, 0:k], ones[0:1, :], grow[:, 0:k], start=True, stop=True).then_inc(max_all, 1)

            across(0, 1)
            back(0, 1)
            for k in range(2 * B * NI):
                kk = k % (B * NI)
                if kk % NI == 0:
                    pe.wait_ge(xq_made, kk // NI + 1)
                if k == 0:
                    pe.wait_ge(x2T_read, B)
                if k >= 6:
                    pe.wait_ge(h_out, k - 5)
                mm(ps[:, k % 6, :], wT[:, k // (B * NI), kk % NI, :], xq[:, kk // NI, :], start=True, stop=True)\
                    .then_inc(h_filled, 1)
                if k == B * NI + 3:
                    across(1, 1)
                if k == B * NI + 4:
                    back(1, 1)
            across(2, 2)
            back(2, 2)
            across(3, 1)
            back(3, 1)
            pe.wait_ge(h_out, 2 * B * NI)
            for b in range(B):
                pe.wait_ge(oq_made, b + 1)
                for t in range(NT):
                    for i in range(NI):
                        last = mm(ps[:, b, P * t:P * (t + 1)], up[:, b, i * T + P * t:i * T + P * (t + 1)], wT[:, 2, i, :],
                                  start=(i == 0), stop=(i == NI - 1))
                last.then_inc(down_filled, 1)


FREED = [sum(j[0] not in ("q", "k", "max_rows") for j in MISC[:n]) for n in range(NMISC + 1)]


def tables():
    f = np.concatenate([np.arange(T // 2 + 1), np.arange(1, T // 2)])
    angle = 2 * np.pi * ((f[None, :] * np.arange(T)[:, None]) % T) / T
    cosines = np.arange(T) <= T // 2
    forward = np.where(cosines[None, :], np.cos(angle), np.sin(angle))
    twice = np.where((f == 0) | (f == T // 2), 1.0, 2.0)
    inverse = (forward * twice[None, :] / T / C).T
    parts = np.array([[n != 0, n == 2] for n in K_PART for _ in range(D)])
    return forward.astype(np.float32), np.ascontiguousarray(inverse.astype(np.float32)), parts.astype(np.float32)


def kernel(x, ctx_1024, L0_attn_Wk, L0_attn_Wv, L0_attn_Wq, L0_attn_Wp, L0_attn_bp, L0_xattn_Wq, L0_xattn_bq, L0_xattn_Wk,
           L0_xattn_bk, L0_xattn_Wv, L0_xattn_bv, L0_xattn_Wo, L0_xattn_bo, L0_ffn_w_gate, L0_ffn_w_up, L0_ffn_w_down):
    import concourse.bacc as bacc
    from concourse.bass_utils import run_bass_kernel_spmd

    dft, idft, parts = tables()
    given = {
        "x": x, "xT": np.asarray(x).reshape(B * T, C).T, "wq": np.asarray(L0_attn_Wq).transpose(1, 0, 2).reshape(C, NH * D),
        "wk": L0_attn_Wk, "wv": L0_attn_Wv, "wp": L0_attn_Wp, "bp": L0_attn_bp,
        "ctxT": np.asarray(ctx_1024).transpose(2, 0, 1),
        "cwq": L0_xattn_Wq, "cwqT": np.asarray(L0_xattn_Wq).T, "cbq": L0_xattn_bq, "cwk": L0_xattn_Wk, "cbk": L0_xattn_bk,
        "cwv": L0_xattn_Wv, "cbv": L0_xattn_bv, "cwo": L0_xattn_Wo, "cbo": L0_xattn_bo,
        "wg": L0_ffn_w_gate, "wu": L0_ffn_w_up, "wd": L0_ffn_w_down, "dft": dft, "idft": idft, "parts": parts,
    }
    nc = bacc.Bacc("TRN2", target_bir_lowering=False, num_devices=1)
    arrays, args = {}, []
    for name, a in given.items():
        a = np.ascontiguousarray(a)
        arrays[f"in_{name}_dram"] = a
        args.append(nc.dram_tensor(f"in_{name}_dram", a.shape, mybir.dt.from_np(a.dtype), kind="ExternalInput").ap())
    args.append(nc.dram_tensor("out_0_dram", (B, T, C), F32, kind="ExternalOutput").ap())
    decoder_layer(nc, *args)
    r = run_bass_kernel_spmd(nc, [arrays], core_ids=[0])
    return r.results[0]["out_0_dram"]
```

```python
from contextlib import ExitStack

import numpy as np

import concourse.bass as bass
from concourse import mybir

F32 = mybir.dt.float32
BF16 = mybir.dt.bfloat16
I16 = mybir.dt.int16
U16 = mybir.dt.uint16
ALU = mybir.AluOpType
ACT = mybir.ActivationFunctionType
AX = mybir.AxisListType

P = 128
B, T, C = 4, 512, 128
NT = T // P
NH, D = 8, 16
S2 = 77
I = 384
NI = I // P
BLK = 32
NB = C // BLK * NI
TOPK = int(2 * np.log(T))
SCALE = C ** -0.5
EPS = 1e-5
QMAX = 32767.0
MAGIC = 1.5 * 2.0 ** 23
LOWEST = -3.0e38
Q_PART = [0, 0, 0, 1, 1, 2]
K_PART = [0, 1, 2, 0, 1, 0]
NS = D * len(Q_PART)
NM = NS + 3
G = 4
STEP = G
UNITS = 3 * NH
ALL_UNITS = B * UNITS
GROUP = UNITS // 2
AHEAD = 3
LAG = 2
RING = 12

MAX_UNITS = [(t, h, n, P * (t + 1)) for t, n in enumerate((4, 2, 1, 1)) for h in range(0, NH, n)]
NMAX = len(MAX_UNITS)
MAX_SLOTS = 15


def side_jobs(n):
    b, u = divmod(n, UNITS)
    jobs = {
        3: [("heads_out", b - 1, 1)],
        4: [("q", b + 2)],
        6: [("attn_turn", b - 1)],
        8: [("attn_proj", b - 1)],
        9: [("k", b + 2)],
        10: [("v", b + 2)],
        13: [("freq", b - 1)],
        16: [("heads_out", b, 0)],
        17: [("max_rows", b + 1)],
        19: [("freq_sum", b - 1)],
    }.get(u, [])
    return [j for j in jobs if 0 <= j[1] < B]


FREQ_TILES = {13: [0], 14: [1], 15: [2, 3]}


def max_units(b, u):
    if b + 1 >= B or u >= MAX_SLOTS:
        return []
    return range(u * NMAX // MAX_SLOTS, (u + 1) * NMAX // MAX_SLOTS)


FIRST_JOBS = [("q", 0), ("k", 0), ("v", 0), ("ctx_k",), ("ctx_vT",)]
BESIDE_JOBS = [("ctx_kf", 0), ("q", 1), ("w_turn", 0), ("k", 1), ("ctx_z", 0), ("v", 1), ("w_turn", 1), ("w_turn", 2),
               ("ctx_vo",), ("ctx_kf", 1), ("ctx_z", 1)]
LATE_JOBS = [("ctx_kf", 2), ("ctx_kf", 3), ("ctx_z", 2), ("ctx_z", 3)]
START_JOBS = FIRST_JOBS + BESIDE_JOBS + [("max_rows", 0)] + LATE_JOBS
TAIL_JOBS = [("heads_out", B - 1, 1), ("attn_turn", B - 1), ("attn_proj", B - 1), ("inverse", 0), ("freq", B - 1),
             ("freq_sum", B - 1), ("inverse", 1)]
DELAY_GROUPS = [range(B - 1), range(B - 1, B)]
MISC = START_JOBS + [j for n in range(ALL_UNITS) for j in side_jobs(n)] \
    + TAIL_JOBS
ORDER = {j: n for n, j in enumerate(MISC)}
START_BANKS = [6, 7, 0, 1, 2, 5]
BANK = [START_BANKS[n % 6] if n < len(START_JOBS) else 6 + n % 2 for n in range(len(MISC))]


def last_on(bank, before):
    return next((n for n in reversed(range(before)) if BANK[n] == bank), None)


def decoder_layer(nc, x_in, xT_in, qkv_in, weights_in, ctxT_in, col_bias_in, row_bias_in, ffn_in, dft_in, idft_in,
                  parts_in, out):
    with ExitStack() as ctx:
        def sb(name, shape, dt=F32):
            return ctx.enter_context(nc.sbuf_tensor(name, shape, dt))

        def sem(name):
            return ctx.enter_context(nc.semaphore(name))

        W = NI * B * T
        early_q, early_p, early_x = sb("early_q", [P, W]), sb("early_p", [P, W]), sb("early_x", [P, W])
        early_w, early_z = sb("early_w", [P, 3 * 3 * NB * BLK]), sb("early_z", [P, B * T])
        bt = "p (b t) -> p b t"
        probs = early_p[:, :].rearrange("p (i q) -> p i q", i=RING)
        early_xT = sb("early_xT", [P, B * T])
        xT, x2 = early_xT[:, :].rearrange(bt, b=B), early_xT[:, :].rearrange("p (b n c) -> p b n c", b=B, n=NT)
        dft, idft = (early_x[:, i * B * T:(i + 1) * B * T].rearrange("p (n t) -> p n t", n=NT) for i in range(2))
        x = early_x[:, 2 * B * T:W].rearrange("p (b n c) -> p b n c", b=B, n=NT)
        qstack = [early_q[:, i * NH * T // 2:(i + 1) * NH * T // 2].bitcast(BF16).rearrange("p (h t) -> p h t", h=NH)
                  for i in range(3)]
        wdiv, wint, wdq = (early_w[:, i * 3 * NB * BLK:(i + 1) * 3 * NB * BLK]
                           .rearrange("p (w k e) -> p w k e", w=3, k=NB) for i in range(3))
        zT = early_z[:, :].rearrange(bt, b=B)
        gate, up = early_q[:, :].rearrange(bt, b=B), early_p[:, :].rearrange(bt, b=B)
        gate16, sig16 = (early_x[:, i * W // 2:(i + 1) * W // 2].bitcast(d).rearrange(bt, b=B)
                         for i, d in enumerate((I16, U16)))
        up16 = early_w[:, 0:W // 2].bitcast(I16).rearrange(bt, b=B)
        xq = early_z[:, :].rearrange(bt, b=B)
        qkv = sb("qkv", [P, (NH + 2) * D])
        wq, wk, wv = qkv[:, 0:NH * D], qkv[:, NH * D:(NH + 1) * D], qkv[:, (NH + 1) * D:(NH + 2) * D]
        wk6 = sb("wk6", [P, D, len(Q_PART)])
        weights = sb("weights", [P, 5, C])
        wp, cwqT, cwk, cwv, cwo = (weights[:, i] for i in range(5))
        row_bias = sb("row_bias", [P, 3, C])
        bp, bo, bk = (row_bias[:, i] for i in range(3))
        parts = sb("parts", [NS, 2])
        ident, identb = sb("ident", [P, P]), sb("identb", [P, P], BF16)
        maskf, maskb = sb("maskf", [P, P]), sb("maskb", [P, P], BF16)
        ones = sb("ones", [P, P])
        warm = sb("warm", [P, T], BF16)
        qpart = [[sb(f"q{n}_{i}", [P, T], BF16) for n in range(3)] for i in range(2)]
        qrest = [sb(f"qrest{i}", [P, T]) for i in range(2)]
        kstack = [sb(f"kstack{i}", [P, T], BF16) for i in range(3)]
        kfirst, krest = sb("kfirst", [NS, T], BF16), sb("krest", [NS, T])
        ksecond = sb("ksecond", [NS, T], BF16)
        vaug = [sb(f"vaug{i}", [P, NT, 32]) for i in range(3)]
        mneg = sb("mneg", [P, NT, NH])
        mrest = sb("mrest", [P, NT, NH])
        mparts = sb("mparts", [P, NT, 3, NH], BF16)
        mrow = [sb(f"mrow{i}", [3 * NH, T], BF16) for i in range(2)]
        headsT = [sb(f"headsT{g}", [P, T]) for g in range(2)]
        sumr = sb("sumr", [P, NT * 4])
        attn = sb("attn", [P, NT, 2, 4, D])
        attnT = sb("attnT", [P, T])
        z1 = sb("z1", [P, NT, C])
        z2, z3 = (a[:, 0:B * T].rearrange("p (b n c) -> p b n c", b=B, n=NT) for a in (early_q, early_x))
        stats, mv = sb("stats", [P, NT, 6]), sb("mv", [P, 3 * B, NT, 2])
        veps, half = sb("veps", [P, NT]), sb("half", [P, NT])
        rstd, shiftn = sb("rstd", [P, 3 * B, NT]), sb("shiftn", [P, 3 * B, NT])
        early_1 = sb("early_1", [P, B * T])
        x1, xround = early_1[:, :].rearrange("p (b n c) -> p b n c", b=B, n=NT), early_1[:, :].rearrange(bt, b=B)
        x1b = sb("x1b", [P, B, NT, C])
        ctxT = sb("ctxT", [P, B, S2])
        col_bias = sb("col_bias", [P, 2])
        bq, bv = col_bias[:, 0:1], col_bias[:, 1:2]
        bqT = sb("bqT", [P, 1])
        ctxk = sb("ctxk", [S2, B, C])
        kfT = [sb(f"kfT{i}", [P, T]) for i in range(2)]
        kf0 = sb("kf0", [P, B, P])
        vT = sb("vT", [P, B, S2])
        vo = sb("vo", [S2, B, C])
        prod = sb("prod", [P, T])
        spec = sb("spec", [P, NT, B])
        corr, corr2, corr3, ecorr = (sb(n, [B, T]) for n in ("corr", "corr2", "corr3", "ecorr"))
        top1, top2, sel = sb("top1", [B, 8]), sb("top2", [B, 8]), sb("sel", [B, 8])
        ntop, wsum, wrec = sb("ntop", [B, 1]), sb("wsum", [B, 1]), sb("wrec", [B, 1])
        wts = sb("wts", [B, T])
        wrap = sb("wrap", [B, T + P])
        shift = [sb(f"shift{b}", [S2, T]) for b in range(B)]
        wraw = sb("wraw", [P, 3, NB, BLK])
        wmax, wscl, winv = (sb(n, [P, 3, NB]) for n in ("wmax", "wscl", "winv"))
        wT = sb("wT", [P, 3, NI, P])
        amax = sb("amax", [P, 4, 16])
        amax1 = sb("amax1", [P, 1])
        gmax = sb("gmax", [P, 1])
        scl = sb("scl", [P, 32])
        scrap = sb("scrap", [P, 1])
        sigp = early_1[:, 0:NI * T]
        y3 = x1

        ps = ctx.enter_context(nc.psum_tensor("ps", [P, 8, T], F32))
        heads = ps[:, 5, :]

        NR = len(Q_PART)
        qdram = nc.dram_tensor("q_parts", [B, NH, D, NR, T], BF16, kind="Internal").ap()

        s_x = [sem(f"x_landed{b}") for b in range(B)]
        s_xn = sem("x_nat_landed")
        s_qkv, s_parts, s_bias = sem("qkv_landed"), sem("parts_landed"), sem("bias_landed")
        wk6_made = sem("wk6_made")
        s_cw = sem("ctx_weights_landed")
        s_dft, s_idft = sem("dft_landed"), sem("idft_landed")
        s_wf = sem("ffn_weights_landed")
        s_const = sem("consts_made")
        s_ident = sem("ident_made")
        warm_made = sem("warm_made")
        misc_filled = sem("misc_filled")
        misc_free = [sem(f"misc_free{n}") for n in range(8)]
        q1_made, q_rest, q2_made, q3_made = sem("q1_made"), sem("q_rest"), sem("q2_made"), sem("q3_made")
        q_in_dram, q_landed = sem("q_in_dram"), [sem(f"q_landed{i}") for i in range(3)]
        k1_made, k_rest, k2_made, k_made = sem("k1_made"), sem("k_rest"), sem("k2_made"), sem("k_made")
        v_made = sem("v_made")
        smax_filled, smax_read = sem("smax_filled"), sem("smax_read")
        mparts_made = sem("mparts_made")
        m_landed = sem("m_landed")
        scores_filled, exp_done, probs_ready, pv_done = (sem(n) for n in ("scores_filled", "exp_done", "probs_ready", "pv_done"))
        heads_read = sem("heads_read")
        attn_made, attnT_made = sem("attn_made"), sem("attnT_made")
        var_made, rstd_made, x1_made, x1b_made = sem("var_made"), sem("rstd_made"), sem("x1_made"), sem("x1b_made")
        xb_made = sem("xb_made")
        ctx_made = sem("ctx_made")
        w_made = sem("w_made")
        prod_made, spec_made = sem("prod_made"), sem("spec_made")
        top_made, ecorr_made = sem("top_made"), sem("ecorr_made")
        wrap_made = sem("wrap_made")
        shift_landed = [sem(f"shift_landed{b}") for b in range(B)]
        agg_filled, agg_read = sem("agg_filled"), sem("agg_read")
        x2_made, x2T_filled, x2T_read, xq_made = sem("x2_made"), sem("x2T_filled"), sem("x2T_read"), sem("xq_made")
        max_col, max_row = sem("max_col"), sem("max_row")
        h_filled, h_out = sem("h_filled"), sem("h_out")
        g16_made, gint_made, sint_made = sem("g16_made"), sem("gint_made"), sem("sint_made")
        hint_made, uint_made = sem("hint_made"), sem("uint_made")
        gmagic_made, hmagic_made, sig_made, s16_made = sem("gmagic_made"), sem("hmagic_made"), sem("sig_made"), sem("s16_made")
        scales_g, scales_h, u16_made, h16_made = sem("scales_g"), sem("scales_h"), sem("u16_made"), sem("h16_made")
        pool_product = sem("pool_product")
        scales_u = sem("scales_u")
        oround_made, oq_made, down_filled, down_read = sem("oround_made"), sem("oq_made"), sem("down_filled"), sem("down_read")
        y_made, y_stored = sem("y_made"), sem("y_stored")
        pool_ch, dve_ch = sem("pool_chain"), sem("dve_chain")

        block = ctx.enter_context(nc.Block())

        BATCHES, BP = (0, 3, 1, 2), 3
        SX, FX, SG, FG, SU, FU, CH, SH, FH, CO, SO, FO, TMP, REC = range(14)

        def col(n):
            return scl[:, n:n + 1]

        def shifted(row):
            a = wrap[row:row + 1, P:P + 1]
            return bass.AP(tensor=a.tensor, offset=a.offset, ap=[a.ap[0], [-1, S2], [1, T]])

        def bank(job):
            return ps[:, BANK[ORDER[job]], :]

        def landed(eng, job):
            eng.wait_ge(misc_filled, ORDER[job] + 1)

        def freed(job):
            return misc_free[BANK[ORDER[job]]]

        def free_count(n):
            return sum(BANK[m] == BANK[n] and MISC[m][0] not in ("q", "k") for m in range(n + 1))

        def done(eng, job):
            eng.wait_ge(freed(job), free_count(ORDER[job]))

        misc = ps[:, 7, :]

        @block.sync
        def _(sp):
            def bounce(b, between=()):
                for n in range(3):
                    sp.wait_ge((q1_made, q2_made, q3_made)[n], b + 1)
                    r, k = Q_PART.index(n), Q_PART.count(n)
                    a = qpart[b % 2][n][:, :]
                    sp.dma_start(qdram[b, :, :, r:r + k, :].rearrange("h d r q -> (h d) r q"),
                                 bass.AP(tensor=a.tensor, offset=a.offset, ap=[a.ap[0], [0, k], [1, T]]))\
                        .then_inc(q_in_dram, 16)
                    for load in between[n:n + 1]:
                        load()
                sp.wait_ge(q_in_dram, 48 * (b + 1))
                if b >= 3:
                    sp.wait_ge(pv_done, UNITS // STEP * (b - 2))
                sp.dma_start(qstack[b % 3][0:NS, :, :], qdram[b].rearrange("h d r q -> (d r) h q"))\
                    .then_inc(q_landed[b % 3], 16)

            def max_rows(b):
                n = ORDER[("max_rows", b)]
                sp.wait_ge(misc_free[BANK[n]], free_count(n))
                sp.dma_start(qstack[b % 3][NS:NM, :, :], mrow[b % 2][:, :]).then_inc(m_landed, 16)

            def load_ffn():
                sp.dma_start(wraw[:, :, :, :].rearrange("p w k e -> p (w k e)"), ffn_in).then_inc(s_wf, 16)

            def load_bias():
                sp.dma_start(row_bias[:, :, :], bass.AP(tensor=row_bias_in.tensor, offset=row_bias_in.offset,
                                                        ap=[[0, P], [C, 3], [1, C]])).then_inc(s_bias, 16)

            def load_dft():
                sp.dma_start(dft[:, :, :], dft_in.rearrange("(n p) f -> p n f", p=P)).then_inc(s_dft, 16)

            sp.dma_start(xT[:, 0, :], xT_in[:, 0:T]).then_inc(s_x[0], 16)
            sp.dma_start(weights[:, :, :].rearrange("p w c -> p (w c)"), weights_in).then_inc(s_cw, 16)
            sp.dma_start(ctxT[:, :, :], ctxT_in).then_inc(s_cw, 16)
            sp.dma_start(col_bias[:, :], col_bias_in).then_inc(s_cw, 16)
            load_bias()
            load_ffn()
            bounce(0, (load_dft,))
            sp.dma_start(xT[:, 1, :], xT_in[:, T:2 * T]).then_inc(s_x[1], 16)
            sp.dma_start(x[:, :, :, :], x_in.rearrange("b (n p) c -> p b n c", p=P)).then_inc(s_xn, 16)
            bounce(1)
            for b in range(2, B):
                sp.dma_start(xT[:, b, :], xT_in[:, b * T:(b + 1) * T]).then_inc(s_x[b], 16)
            sp.dma_start(idft[:, :, :], idft_in.rearrange("(n p) l -> p n l", p=P)).then_inc(s_idft, 16)
            max_rows(0)
            for b in range(B):
                if b + 2 < B:
                    bounce(b + 2)
                if b + 1 < B:
                    max_rows(b + 1)
            sp.wait_ge(wrap_made, 1)
            for b in (0, 2):
                sp.dma_start(shift[b][:, :], shifted(b)).then_inc(shift_landed[b], 16)
            sp.wait_ge(wrap_made, 2)
            sp.dma_start(shift[B - 1][:, :], shifted(0)).then_inc(shift_landed[B - 1], 16)
            for b in range(B):
                sp.wait_ge(y_made, b + 1)
                sp.dma_start(out[b].rearrange("(n p) c -> p n c", p=P), y3[:, b]).then_inc(y_stored, 16)
            sp.wait_ge(y_stored, 16 * B)

        @block.gpsimd
        def _(pool):
            chain = [0]

            def link(ins):
                chain[0] += 1
                ins.then_inc(pool_ch, 1)
                pool.wait_ge(pool_ch, chain[0])

            g = nc.gpsimd
            g.memset(ones[:, :], 1.0)
            link(g.memset(ident[:, :], 0.0))
            g.affine_select(out=ident[:, :], in_=ident[:, :], compare_op=ALU.not_equal, fill=1.0, base=0,
                            pattern=[[-1, P]], channel_multiplier=1).then_inc(s_ident, 1)
            link(g.memset(maskf[:, :], 0.0))
            link(g.affine_select(out=maskf[:, :], in_=maskf[:, :], compare_op=ALU.is_ge, fill=LOWEST, base=0,
                                 pattern=[[-1, P]], channel_multiplier=1))
            g.tensor_copy(maskb[:, :], maskf[:, :])
            pool.wait_ge(s_ident, 1)
            for i in range(3):
                link(g.memset(vaug[i][:, :, :], 0.0))
                g.memset(vaug[i][:, :, D:D + 1], 1.0)
            g.memset(half[:, :], -0.5)
            g.tensor_copy(identb[:, :], ident[:, :]).then_inc(s_const, 1)

            def q_third(b):
                pool.wait_ge(q2_made, b + 1)
                if b >= 2:
                    pool.wait_ge(q_in_dram, 48 * (b - 1))
                g.tensor_tensor(qpart[b % 2][2][:, :], qrest[b % 2][:, :], qpart[b % 2][1][:, :], ALU.subtract)\
                    .then_inc(q3_made, 1)

            def inv_std(n):
                pool.wait_ge(var_made, n + 1)
                link(g.tensor_scalar(veps[:, :], mv[:, n, :, 1], EPS, None, ALU.add))
                if n < B:
                    g.tensor_tensor(rstd[:, n], veps[:, :], half[:, :], ALU.pow).then_inc(rstd_made, 1)
                    return
                link(g.tensor_tensor(rstd[:, n], veps[:, :], half[:, :], ALU.pow))
                link(g.tensor_tensor(shiftn[:, n], mv[:, n, :, 0], rstd[:, n], ALU.mult))
                g.tensor_scalar(shiftn[:, n], shiftn[:, n], -1.0, None, ALU.mult).then_inc(rstd_made, 1)

            def add_bo(b):
                pool.wait_ge(x1_made, b + 1)
                g.tensor_tensor(x1b[:, b], x1[:, b], bo_b, ALU.add).then_inc(x1b_made, 1)

            bo_b = bass.AP(tensor=bo[:, :].tensor, offset=bo[:, :].offset, ap=[bo[:, :].ap[0], [0, NT], [1, C]])
            bp_b = bass.AP(tensor=bp[:, :].tensor, offset=bp[:, :].offset, ap=[bp[:, :].ap[0], [0, NT], [1, C]])

            def select(i):
                pool.wait_ge(exp_done, STEP * (i + 1))
                pt = probs[:, STEP * i % RING:STEP * i % RING + STEP, :]
                if i % 3 < 2:
                    v, pattern = pt[:, :, 0:P], [[0, STEP], [1, P]]
                else:
                    v = pt.rearrange("p h (j q) -> p h j q", q=2 * P)[:, :, :, 0:P]
                    pattern = [[0, STEP], [0, 2], [1, P]]
                g.affine_select(out=v, in_=v, compare_op=ALU.is_ge, fill=0.0, base=0, pattern=pattern,
                                channel_multiplier=-1).then_inc(probs_ready, 1)

            q_third(0)
            q_third(1)
            pool.wait_ge(s_cw, 48)
            g.tensor_scalar(bqT[:, :], bq[:, :], float(T), None, ALU.mult).then_inc(ctx_made, 1)
            pool.wait_ge(s_bias, 16)
            pool.wait_ge(s_xn, 16)
            for b in range(B):
                g.tensor_tensor(x[:, b], x[:, b], bp_b, ALU.add).then_inc(xb_made, 1)
            for b in range(B):
                for u in range(UNITS):
                    n = b * UNITS + u
                    if n % STEP == 0:
                        select(n // STEP)
                    if u == 8 and b + 2 < B:
                        q_third(b + 2)
                    if u == 9 and b >= 1:
                        inv_std(b - 1)
                    if u == 13 and b >= 1:
                        add_bo(b - 1)
            inv_std(B - 1)
            add_bo(B - 1)
            for n in range(B, 2 * B):
                inv_std(n)
            pool.wait_ge(sint_made, 1)
            g.tensor_tensor(gate[:, BP], gate[:, BP], sigp[:, :], ALU.mult).then_inc(pool_product, 1)
            pool.wait_ge(hint_made, 1)
            pool.wait_ge(uint_made, 1)
            g.tensor_tensor(gate[:, BP], gate[:, BP], up[:, BP], ALU.mult).then_inc(pool_product, 1)
            for n in range(2 * B, 3 * B):
                inv_std(n)

        @block.scalar
        def _(act):
            s = nc.scalar
            act.dma_start(qkv[:, :], qkv_in).then_inc(s_qkv, 16)
            act.dma_start(parts[:, :], parts_in).then_inc(s_parts, 16)
            act.wait_ge(s_const, 2)
            s.activation(scrap[:, 0:1], half[:, 0:1], ACT.Exp)

            def exps(n):
                act.wait_ge(scores_filled, n + 1)
                if n >= RING:
                    act.wait_ge(pv_done, (n - RING) // STEP + 1)
                w = T if n // STEP % 3 == 0 else T - P
                s.activation(probs[:, n % RING, 0:w], ps[:, n % AHEAD, 0:w], ACT.Exp, scale=SCALE).then_inc(exp_done, 1)

            def heads_evict(k):
                act.wait_ge(pv_done, 3 * (k + 1))
                if k >= 2:
                    act.wait_ge(misc_filled, ORDER[("heads_out", k // 2 - 1, k % 2)] + 1)
                s.activation(headsT[k % 2][:, :], heads, ACT.Copy).then_inc(heads_read, 1)

            def side(job):
                kind = job[0]
                src = bank(job)
                if kind == "q":
                    b = job[1]
                    if b >= 2:
                        act.wait_ge(q_in_dram, 48 * (b - 1))
                    landed(act, job)
                    s.activation(qpart[b % 2][0][:, :], src, ACT.Copy).then_inc(q1_made, 1)
                elif kind == "k":
                    b = job[1]
                    if b >= 1:
                        act.wait_ge(k_rest, b)
                    landed(act, job)
                    s.activation(kfirst[:, :], src[0:NS, :], ACT.Copy).then_inc(k1_made, 1)
                elif kind == "v":
                    b = job[1]
                    landed(act, job)
                    if b >= 3:
                        act.wait_ge(pv_done, UNITS // STEP * (b - 2))
                    s.activation(vaug[b % 3][:, :, 0:D], src[:, 0:NT * D].rearrange("p (n d) -> p n d", n=NT),
                                 ACT.Copy).then_inc(freed(job), 1)
                elif kind == "max_rows":
                    b = job[1]
                    landed(act, job)
                    if b >= 2:
                        act.wait_ge(m_landed, 16 * (b - 1))
                    s.activation(mrow[b % 2][:, :], src[0:3 * NH, :], ACT.Copy).then_inc(freed(job), 1)
                elif kind == "attn_turn":
                    landed(act, job)
                    if job[1] >= 1:
                        act.wait_ge(misc_filled, ORDER[("attn_proj", job[1] - 1)] + 1)
                    s.activation(attnT[:, :], src, ACT.Copy).then_inc(freed(job), 1)
                elif kind == "freq_sum":
                    landed(act, job)
                    s.activation(spec[:, :, job[1]], src[:, 0:NT], ACT.Copy).then_inc(freed(job), 1)
                elif kind == "ctx_vT":
                    landed(act, job)
                    act.wait_ge(s_cw, 48)
                    s.activation(vT[:, :, :], src[:, 0:B * S2].rearrange("p (b s) -> p b s", b=B), ACT.Identity,
                                 bias=bv[:, 0:1]).then_inc(freed(job), 1)
                elif kind == "w_turn":
                    landed(act, job)
                    s.activation(wT[:, job[1]], src[:, 0:NI * P].rearrange("p (i o) -> p i o", i=NI), ACT.Copy)\
                        .then_inc(freed(job), 1)
                elif kind == "ctx_kf":
                    b = job[1]
                    landed(act, job)
                    if b >= 2:
                        act.wait_ge(misc_filled, ORDER[("ctx_z", b - 2)] + 1)
                    s.activation(kf0[:, b, 0:1], src[:, 0:1], ACT.Copy)
                    s.activation(kfT[b % 2][:, :], src, ACT.Copy).then_inc(freed(job), 1)
                elif kind == "ctx_z":
                    landed(act, job)
                    s.activation(zT[:, job[1], :], src, ACT.Copy).then_inc(freed(job), 1)
                elif kind == "ctx_vo":
                    landed(act, job)
                    s.activation(vo[:, :, :], src[0:S2, :].rearrange("p (b c) -> p b c", b=B), ACT.Copy)\
                        .then_inc(freed(job), 1)

            def second_part(job):
                kind, b = job[0], job[1]
                if kind == "q":
                    act.wait_ge(q_rest, b + 1)
                    s.activation(qpart[b % 2][1][:, :], qrest[b % 2][:, :], ACT.Copy).then_inc(q2_made, 1)
                elif kind == "k":
                    act.wait_ge(k_rest, b + 1)
                    if b >= 1:
                        act.wait_ge(k_made, b)
                    s.activation(ksecond[:, :], krest[:, :], ACT.Copy).then_inc(k2_made, 1)

            for n, job in enumerate(START_JOBS):
                side(job)
                if n > 0 and START_JOBS[n - 1][0] in ("q", "k"):
                    second_part(START_JOBS[n - 1])
            for n in range(AHEAD):
                exps(n)
            for b in range(B):
                for u in range(UNITS):
                    n = b * UNITS + u
                    if n + AHEAD < ALL_UNITS:
                        exps(n + AHEAD)
                    if n >= LAG and (n - LAG) % GROUP == GROUP - 1:
                        heads_evict((n - LAG) // GROUP)
                    for job in side_jobs(n - 1):
                        side(job)
                    for job in side_jobs(n - 3):
                        if job[0] in ("q", "k"):
                            second_part(job)
            heads_evict(2 * B - 1)
            def delay_exp(g):
                n = len(DELAY_GROUPS[g])
                act.wait_ge(top_made, g + 1)
                s.activation(ecorr[0:n, :], corr[0:n, :], ACT.Exp, bias=ntop[0:n, 0:1]).then_inc(ecorr_made, 1)

            for job in TAIL_JOBS:
                if job == ("inverse", 0):
                    delay_exp(0)
                else:
                    side(job)
            act.wait_ge(wrap_made, 1)
            act.dma_start(shift[1][:, :], shifted(1)).then_inc(shift_landed[1], 16)
            delay_exp(1)

            def normalise(n, src, dst, made):
                act.wait_ge(rstd_made, n + 1)
                for t in range(NT):
                    ins = s.activation(dst[:, n % B, t, :], src[:, n % B, t, :], ACT.Identity,
                                       bias=shiftn[:, n, t:t + 1], scale=rstd[:, n, t:t + 1])
                ins.then_inc(made, 1)

            for b in range(B):
                normalise(B + b, z2, x2, x2_made)
            for b in range(B):
                act.wait_ge(x2T_read, b + 1)
                s.activation(xq[:, b], xround[:, b], ACT.Copy, bias=-MAGIC).then_inc(xq_made, 1)

            def hidden_out(k):
                hid = gate if k < B * NI else up
                kk = k % (B * NI)
                act.wait_ge(h_filled, k + 1)
                s.activation(hid[:, kk // NI, (kk % NI) * T:(kk % NI + 1) * T], ps[:, k % 6, :], ACT.Copy).then_inc(h_out, 1)

            for k in range(B * NI):
                hidden_out(k)
            s.activation(scrap[:, 0:1], half[:, 0:1], ACT.Sigmoid)
            k = B * NI
            for n, b in enumerate(BATCHES):
                while k < min(B + n + 2, 2 * B) * NI:
                    hidden_out(k)
                    k += 1
                if b == BP:
                    act.wait_ge(gmagic_made, 1)
                    s.activation(gate[:, b], gate[:, b], ACT.Copy, bias=-MAGIC).then_inc(gint_made, 1)
                    act.wait_ge(gint_made, 1)
                    s.activation(sigp[:, :], gate[:, b], ACT.Sigmoid, scale=col(SG)).then_inc(sig_made, 1)
                    continue
                if n > 0:
                    act.wait_ge(scales_g, 1)
                    s.activation(gate16[:, b], gate[:, b], ACT.Copy, scale=col(FG)).then_inc(g16_made, 1)
                act.wait_ge(g16_made, 1 if n == 0 else n)
                s.activation(gate[:, b], gate16[:, b], ACT.Sigmoid, scale=col(SG)).then_inc(sig_made, 1)
                if n == BATCHES.index(BP) + 1:
                    act.wait_ge(s16_made, n)
                    s.activation(sigp[:, :], sig16[:, BP], ACT.Copy).then_inc(sint_made, 1)
            act.wait_ge(scales_u, 1)
            for b in BATCHES:
                s.activation(up16[:, b], up[:, b], ACT.Copy, scale=col(FU)).then_inc(u16_made, 1)
                if b == BP:
                    act.wait_ge(u16_made, BATCHES.index(b) + 1)
                    s.activation(up[:, b], up16[:, b], ACT.Copy).then_inc(uint_made, 1)
            act.wait_ge(hmagic_made, 1)
            s.activation(gate[:, BP], gate[:, BP], ACT.Copy, bias=-MAGIC).then_inc(hint_made, 1)
            act.wait_ge(scales_h, 1)
            for b in BATCHES[2:]:
                s.activation(gate16[:, b], gate[:, b], ACT.Copy, scale=col(FH)).then_inc(h16_made, 1)
            for b in range(B):
                act.wait_ge(oround_made, b + 1)
                s.activation(up[:, b], gate[:, b], ACT.Copy, bias=-MAGIC).then_inc(oq_made, 1)
            for b in range(B):
                normalise(2 * B + b, z3, y3, y_made)

        @block.vector
        def _(dve):
            v = nc.vector
            chain = [0]

            def link(ins):
                chain[0] += 1
                ins.then_inc(dve_ch, 1)
                dve.wait_ge(dve_ch, chain[0])

            def max_unit(b, i):
                t, h, n, w = MAX_UNITS[i]
                m = NMAX * b + i
                dve.wait_ge(smax_filled, m + 1)
                v.tensor_reduce(mneg[:, t, h:h + n], ps[:, 3 + m % 2, 0:n * w].rearrange("p (h s) -> p h s", h=n),
                                AX.X, ALU.max, negate=True).then_inc(smax_read, 1)
                if i == NMAX - 1:
                    if b >= 1:
                        dve.wait_ge(misc_filled, ORDER[("max_rows", b - 1)] + 1)
                    dve.wait_ge(smax_read, NMAX * (b + 1))
                    link(v.tensor_copy(mparts[:, :, 0, :], mneg[:, :, :]))
                    link(v.tensor_tensor(mrest[:, :, :], mneg[:, :, :], mparts[:, :, 0, :], ALU.subtract))
                    link(v.tensor_copy(mparts[:, :, 1, :], mrest[:, :, :]))
                    v.tensor_tensor(mparts[:, :, 2, :], mrest[:, :, :], mparts[:, :, 1, :], ALU.subtract)\
                        .then_inc(mparts_made, 1)

            def norm_stats(n, z):
                for t in range(NT):
                    ins = v.bn_stats(stats[:, t, :], z[:, t, :])
                link(ins)
                for t in range(NT):
                    ins = v.bn_aggr(mv[:, n, t, :], stats[:, t, :])
                ins.then_inc(var_made, 1)

            def normalise(n, dst):
                dve.wait_ge(rstd_made, n + 1)
                dve.wait_ge(var_made, n + 1)
                for t in range(NT):
                    ins = v.tensor_scalar(dst[:, t, :], z1[:, t, :], mv[:, n, t, 0:1], rstd[:, n, t:t + 1],
                                          ALU.subtract, ALU.mult)
                return ins

            bk_b = bass.AP(tensor=bk[:, :].tensor, offset=bk[0:S2, :].offset, ap=[bk[0:S2, :].ap[0], [0, B], [1, C]])

            def side(job):
                kind = job[0]
                src = bank(job)
                if kind == "q":
                    b = job[1]
                    if b >= 2:
                        dve.wait_ge(q3_made, b - 1)
                    dve.wait_ge(q1_made, b + 1)
                    v.tensor_tensor(qrest[b % 2][:, :], src, qpart[b % 2][0][:, :], ALU.subtract).then_inc(q_rest, 1)
                elif kind == "k":
                    b = job[1]
                    if b >= 1:
                        dve.wait_ge(k2_made, b)
                        dve.wait_ge(k_made, b)
                    dve.wait_ge(k1_made, b + 1)
                    v.scalar_tensor_tensor(krest[:, :], kfirst[:, :], parts[:, 0:1], src[0:NS, :],
                                           ALU.mult, ALU.subtract).then_inc(k_rest, 1)
                elif kind == "heads_out":
                    _, b, g = job
                    landed(dve, job)
                    if g == 0 and b >= 1:
                        dve.wait_ge(misc_filled, ORDER[("attn_turn", b - 1)] + 1)
                    link(v.reciprocal(sumr[:, :], src.rearrange("p (k e) -> p k e", e=32)[:, :, D]))
                    rec = sumr[:, :]
                    rec = bass.AP(tensor=rec.tensor, offset=rec.offset, ap=[rec.ap[0], [4, NT], [1, 4], [0, D]])
                    v.tensor_tensor(attn[:, :, g], src.rearrange("p (t h e) -> p t h e", t=NT, h=4)[:, :, :, 0:D], rec,
                                    ALU.mult).then_inc(freed(job), 1)
                elif kind == "attn_proj":
                    b = job[1]
                    landed(dve, job)
                    dve.wait_ge(xb_made, b + 1)
                    dve.wait_ge(x1_made, b)
                    v.tensor_tensor(z1[:, :, :], src.rearrange("p (t c) -> p t c", t=NT), x[:, b], ALU.add)\
                        .then_inc(freed(job), 1)
                    dve.wait_ge(freed(job), free_count(ORDER[job]))
                    norm_stats(b, z1)
                elif kind == "freq":
                    b = job[1]
                    landed(dve, job)
                    if b >= 1:
                        dve.wait_ge(misc_filled, ORDER[("freq_sum", b - 1)] + 1)
                    v.tensor_tensor(prod[:, :], src, zT[:, b, :], ALU.mult).then_inc(freed(job), 1)
                elif kind == "ctx_k":
                    landed(dve, job)
                    dve.wait_ge(s_bias, 16)
                    v.tensor_tensor(ctxk[:, :, :], src[0:S2, :].rearrange("p (b c) -> p b c", b=B), bk_b, ALU.add)\
                        .then_inc(freed(job), 1)

            def k_last(b):
                dve.wait_ge(k2_made, b + 1)
                if b >= 3:
                    dve.wait_ge(pv_done, UNITS // STEP * (b - 2))
                v.scalar_tensor_tensor(kstack[b % 3][0:NS, :], ksecond[:, :], parts[:, 1:2], krest[:, :],
                                       ALU.mult, ALU.subtract).then_inc(k_made, 1)

            v.memset(warm[:, :], 1.0).then_inc(warm_made, 1)
            dve.wait_ge(s_qkv, 16)
            a = wk[:, :]
            v.tensor_copy(wk6[:, :, :], bass.AP(tensor=a.tensor, offset=a.offset, ap=[a.ap[0], [1, D], [0, NR]]))\
                .then_inc(wk6_made, 1)
            ins = v.memset(kf0[:, :, :], 0.0)
            ins.then_inc(s_const, 1)
            for i in range(3):
                v.memset(kstack[i][NS:NS + 32, :], 1.0)
            dve.wait_ge(s_parts, 16)
            for job in FIRST_JOBS:
                side(job)
                if job[0] == "k":
                    k_last(job[1])
            dve.wait_ge(s_wf, 16)
            w3 = wraw[:, :, :, :].rearrange("p w k e -> p (w k) e")
            link(v.tensor_reduce(wmax[:, :, :].rearrange("p w k -> p (w k)"), w3, AX.X, ALU.max, apply_absolute_value=True))
            link(v.tensor_scalar(wscl[:, :, :], wmax[:, :, :], 1.0 / 7.0, 1e-12, ALU.mult, ALU.max))
            link(v.reciprocal(winv[:, :, :], wscl[:, :, :]))
            sw, iw = (bass.AP(tensor=a.tensor, offset=a.offset, ap=[a.ap[0], [1, 3 * NB], [0, BLK]])
                      for a in (wscl[:, :, :], winv[:, :, :]))
            flat = "p w k e -> p (w k) e"
            link(v.tensor_tensor(wdiv[:, :, :, :].rearrange(flat), w3, iw, ALU.mult))
            link(v.tensor_scalar(wint[:, :, :, :], wdiv[:, :, :, :], MAGIC, MAGIC, ALU.add, ALU.subtract))
            link(v.tensor_scalar(wdiv[:, :, :, :], wint[:, :, :, :], -8.0, 7.0, ALU.max, ALU.min))
            v.tensor_tensor(wdq[:, :, :, :].rearrange(flat), wdiv[:, :, :, :].rearrange(flat), sw, ALU.mult)\
                .then_inc(w_made, 1)
            for i in range(NMAX):
                max_unit(0, i)
                if i % 2 == 0 and i > 0:
                    job = BESIDE_JOBS[i // 2 - 1]
                    if job[0] in ("q", "k"):
                        side(job)
                if i % 2 == 1 and BESIDE_JOBS[i // 2 - 1][0] == "k":
                    k_last(BESIDE_JOBS[i // 2 - 1][1])
            for b in range(B):
                for u in range(UNITS):
                    n = b * UNITS + u
                    for i in max_units(b, u):
                        max_unit(b + 1, i)
                    for job in side_jobs(n - 1):
                        if job[0] in ("heads_out", "attn_proj"):
                            side(job)
                    for job in side_jobs(n - 2):
                        if job[0] in ("q", "k"):
                            side(job)
                    if u == 16 and b >= 1:
                        side(("freq", b - 1))
                    if u == 13 and b + 2 < B:
                        k_last(b + 2)
                    if b >= 1 and u == 11:
                        normalise(b - 1, x1[:, b - 1]).then_inc(x1_made, 1)
            for job in TAIL_JOBS[:3]:
                side(job)
            normalise(B - 1, x1[:, B - 1]).then_inc(x1_made, 1)

            def largest_delays(g):
                n = len(DELAY_GROUPS[g])
                landed(dve, ("inverse", g))
                v.tensor_copy(corr[0:n, :], bank(("inverse", g))[0:n, :]).then_inc(freed(("inverse", g)), 1)
                done(dve, ("inverse", g))
                link(v.max(top1[0:n, :], corr[0:n, :]))
                v.tensor_scalar(ntop[0:n, :], top1[0:n, 0:1], -1.0, None, ALU.mult).then_inc(top_made, 1)
                link(v.match_replace(corr2[0:n, :], top1[0:n, :], corr[0:n, :], LOWEST))
                link(v.max(top2[0:n, :], corr2[0:n, :]))

            def delay_weights(g):
                n = len(DELAY_GROUPS[g])
                v.tensor_copy(sel[0:n, 0:TOPK - 8], top2[0:n, 0:TOPK - 8])
                link(v.memset(sel[0:n, TOPK - 8:8], LOWEST))
                link(v.match_replace(corr3[0:n, :], sel[0:n, :], corr2[0:n, :], LOWEST))
                dve.wait_ge(ecorr_made, g + 1)
                link(v.scalar_tensor_tensor(wts[0:n, :], corr3[0:n, :], LOWEST, ecorr[0:n, :], ALU.is_equal, ALU.mult,
                                            accum_out=wsum[0:n, :]))
                link(v.reciprocal(wrec[0:n, :], wsum[0:n, :]))
                if g > 0:
                    for b in DELAY_GROUPS[g - 1]:
                        dve.wait_ge(shift_landed[b], 16)
                a = wts[0:n, :]
                back = bass.AP(tensor=a.tensor, offset=a.offset + T - 1, ap=[a.ap[0], [-1, T - 1]])
                v.tensor_scalar(wrap[0:n, P + 1:P + T], back, wrec[0:n, 0:1], None, ALU.mult)
                v.tensor_scalar(wrap[0:n, P:P + 1], wts[0:n, 0:1], wrec[0:n, 0:1], None, ALU.mult)
                back = bass.AP(tensor=a.tensor, offset=a.offset + P, ap=[a.ap[0], [-1, P]])
                v.tensor_scalar(wrap[0:n, 0:P], back, wrec[0:n, 0:1], None, ALU.mult).then_inc(wrap_made, 1)

            largest_delays(0)
            side(("freq", B - 1))
            delay_weights(0)
            largest_delays(1)
            delay_weights(1)

            def largest_x2(b):
                dve.wait_ge(x2_made, b + 1)
                return v.tensor_reduce(amax[:, 0, b:b + 1], x2[:, b].rearrange("p t c -> p (t c)"), AX.X, ALU.max,
                                       apply_absolute_value=True)

            for b in range(B):
                dve.wait_ge(agg_filled, b + 1)
                dve.wait_ge(x1b_made, b + 1)
                link(v.tensor_tensor(z2[:, b], ps[:, b, :].rearrange("p (t c) -> p t c", t=NT), x1b[:, b], ALU.add))
                norm_stats(B + b, z2[:, b])
                if b >= 2:
                    largest_x2(b - 2)
            for b in range(B - 2, B):
                last = largest_x2(b)
            link(last)

            def column(row, count):
                v.tensor_reduce(amax1[:, :], amax[:, row, 0:count], AX.X, ALU.max).then_inc(max_col, 1)

            def largest(n):
                dve.wait_ge(max_row, n + 1)
                link(v.tensor_reduce(gmax[:, :], misc[:, 0:P], AX.X, ALU.max))

            def scale_of(c, s_out, f_out, ready=None):
                link(v.tensor_scalar(col(s_out), gmax[:, :], 1.0 / QMAX if c is None else col(TMP), 1e-12, ALU.mult, ALU.max))
                ins = v.reciprocal(col(f_out if c is None else REC), col(s_out))
                if c is not None:
                    link(ins)
                    ins = v.tensor_tensor(col(f_out), col(REC), col(c), ALU.mult)
                if ready is None:
                    link(ins)
                else:
                    ins.then_inc(ready, 1)
                    dve.wait_ge(ready, 1)

            def over_qmax(c):
                link(v.tensor_scalar(col(TMP), col(c), 1.0 / QMAX, None, ALU.mult))

            column(0, B)
            largest(0)
            scale_of(None, SX, FX)
            for b in range(B):
                dve.wait_ge(x2T_filled, b + 1)
                v.tensor_scalar(xround[:, b], ps[:, [4, 5, 6, 0][b], :], col(FX), MAGIC, ALU.mult, ALU.add)\
                    .then_inc(x2T_read, 1)
            over_qmax(SX)

            def hidden_max(hid, row, k):
                kk = k % (B * NI)
                dve.wait_ge(h_out, k + 1)
                return v.tensor_reduce(amax[:, row, kk:kk + 1], hid[:, kk // NI, (kk % NI) * T:(kk % NI + 1) * T], AX.X, ALU.max,
                                       apply_absolute_value=True)

            def batch_max(row, b):
                return v.tensor_reduce(amax[:, row, b:b + 1], gate[:, b], AX.X, ALU.max, apply_absolute_value=True)

            for k in range(B * NI):
                last = hidden_max(gate, 0, k)
            link(last)
            column(0, B * NI)
            hidden_max(up, 1, B * NI)
            largest(1)
            scale_of(SX, SG, FG, scales_g)
            v.tensor_scalar(gate16[:, BATCHES[0]], gate[:, BATCHES[0]], col(FG), None, ALU.mult).then_inc(g16_made, 1)
            v.tensor_scalar(gate[:, BP], gate[:, BP], col(FG), MAGIC, ALU.mult, ALU.add).then_inc(gmagic_made, 1)
            link(v.tensor_scalar(col(CH), col(SG), 1.0 / 65536.0, None, ALU.mult))
            for n, b in enumerate(BATCHES):
                for i in range(n == 0, NI):
                    ins = hidden_max(up, 1, (B + n) * NI + i)
                if n == B - 1:
                    link(ins)
                    column(1, B * NI)
                dve.wait_ge(sig_made, n + 1)
                v.tensor_scalar(sig16[:, b], sigp[:, :] if b == BP else gate[:, b], 65536.0, 65535.0, ALU.mult, ALU.min)\
                    .then_inc(s16_made, 1)
                if b == BP:
                    continue
                if n == B - 1:
                    largest(2)
                    scale_of(SX, SU, FU)
                    v.tensor_copy(col(CO), col(SU)).then_inc(scales_u, 1)
                dve.wait_ge(s16_made, n + 1)
                link(v.tensor_tensor(gate[:, b], gate16[:, b], sig16[:, b], ALU.mult))
                batch_max(2, b)
            dve.wait_ge(pool_product, 1)
            link(batch_max(2, BP))
            column(2, B)
            over_qmax(CH)
            largest(3)
            scale_of(CH, SH, FH, scales_h)
            v.tensor_scalar(gate[:, BP], gate[:, BP], col(FH), MAGIC, ALU.mult, ALU.add).then_inc(hmagic_made, 1)
            link(v.tensor_scalar(gate16[:, BATCHES[0]], gate[:, BATCHES[0]], col(FH), None, ALU.mult))
            dve.wait_ge(scales_u, 1)
            link(v.tensor_tensor(col(CO), col(SH), col(SU), ALU.mult))
            for n, b in enumerate(b for b in BATCHES if b != BP):
                if n > 0:
                    dve.wait_ge(h16_made, n)
                dve.wait_ge(u16_made, BATCHES.index(b) + 1)
                link(v.tensor_tensor(gate[:, b], gate16[:, b], up16[:, b], ALU.mult))
                batch_max(0, b)
            dve.wait_ge(pool_product, 2)
            link(batch_max(0, BP))
            column(0, B)
            over_qmax(CO)
            largest(4)
            scale_of(CO, SO, FO)
            for b in range(B):
                v.tensor_scalar(gate[:, b], gate[:, b], col(FO), MAGIC, ALU.mult, ALU.add).then_inc(oround_made, 1)
            for b in range(B):
                dve.wait_ge(down_filled, b + 1)
                link(v.scalar_tensor_tensor(z3[:, b].rearrange("p t c -> p (t c)"), ps[:, b, :], col(SO),
                                            x2[:, b].rearrange("p t c -> p (t c)"), ALU.mult, ALU.add))
                norm_stats(2 * B + b, z3[:, b])

        @block.tensor
        def _(pe):
            mm = nc.tensor.matmul

            def warm_up(bank, count):
                for _ in range(count):
                    mm(ps[:, bank, :], warm[:, 0:P], warm[:, :], start=True, stop=True)

            def score_unit(n):
                b, u = divmod(n, UNITS)
                i, hh = divmod(u, STEP)
                h, kind = i // 3 * G + hh, i % 3
                if n >= AHEAD:
                    pe.wait_ge(exp_done, n - AHEAD + 1)
                else:
                    m = last_on(n, len(START_JOBS))
                    pe.wait_ge(misc_free[n], free_count(m))
                if u == 0:
                    warm_up(n % AHEAD, 6)
                    pe.wait_ge(m_landed, 16 * (b + 1))
                q, k, sc = qstack[b % 3], kstack[b % 3], ps[:, n % AHEAD, :]
                if kind < 2:
                    last = mm(sc[:, 0:T - P * kind], k[0:NM, P * kind:P * (kind + 1)], q[0:NM, h, P * kind:T],
                              start=True, stop=True)
                else:
                    mm(sc[:, 0:2 * P], k[0:NM, 2 * P:3 * P], q[0:NM, h, 2 * P:T], start=True, stop=True)
                    last = mm(sc[:, 2 * P:3 * P], k[0:NM, 3 * P:T], q[0:NM, h, 3 * P:T], start=True, stop=True)
                last.then_inc(scores_filled, 1)

            def value_step(i):
                b, kind = i // (UNITS // STEP), i % 3
                pe.wait_ge(probs_ready, i + 1)
                if i == 0:
                    pe.wait_ge(misc_free[5], free_count(last_on(5, len(START_JOBS))))
                elif kind == 0:
                    pe.wait_ge(heads_read, i // 3)
                if i % (UNITS // STEP) == 0:
                    done(pe, ("v", b))
                va = vaug[b % 3]
                for j in ((0,), (1,), (2, 3))[kind]:
                    for hh in range(G):
                        pt = probs[:, (STEP * i + hh) % RING, :]
                        pt = pt[:, 2 * P:3 * P] if j == 3 else pt[:, 0:T - P * j]
                        last = mm(heads[32 * hh:32 * hh + 32, P * j:T], va[:, j, :], pt, start=(j == 0), stop=(j == 3))
                last.then_inc(pv_done, 1)

            def max_unit(b, i):
                t, h0, n, w = MAX_UNITS[i]
                if i == 0:
                    pe.wait_ge(q_landed[b % 3], 16 * (b // 3 + 1))
                    pe.wait_ge(k_made, b + 1)
                m = NMAX * b + i
                if m >= 2:
                    pe.wait_ge(smax_read, m - 1)
                for h in range(n):
                    o = ps[:, 3 + m % 2, h * w:(h + 1) * w]
                    mm(o, qstack[b % 3][0:NS, h0 + h, P * t:P * (t + 1)], kstack[b % 3][0:NS, 0:w], start=True, stop=False)
                    last = mm(o[:, w - P:w], identb[:, :], maskb[:, :], start=False, stop=True)
                last.then_inc(smax_filled, 1)

            def freq(job, tiles):
                if tiles[0] == 0:
                    waits_for_bank(ORDER[job])
                    pe.wait_ge(x1_made, job[1] + 1)
                for t in tiles:
                    last = mm(bank(job), x1[:, job[1], t, :], dft[:, t, :], start=(t == 0), stop=(t == NT - 1))
                if t == NT - 1:
                    last.then_inc(misc_filled, 1)

            def side(job):
                n, kind = ORDER[job], job[0]
                misc = bank(job)
                waits_for_bank(n)
                if kind == "q":
                    pe.wait_ge(s_qkv, 16)
                    pe.wait_ge(s_x[job[1]], 16)
                    last = mm(misc, wq[:, :], xT[:, job[1], :], start=True, stop=True)
                elif kind == "k":
                    pe.wait_ge(wk6_made, 1)
                    last = mm(misc[0:NS, :], wk6[:, :, :].rearrange("p d r -> p (d r)"), xT[:, job[1], :],
                              start=True, stop=True)
                elif kind == "v":
                    pe.wait_ge(s_qkv, 16)
                    for t in range(NT):
                        last = mm(misc[:, t * D:(t + 1) * D], xT[:, job[1], P * t:P * (t + 1)], wv[:, :],
                                  start=True, stop=True)
                elif kind == "max_rows":
                    pe.wait_ge(mparts_made, job[1] + 1)
                    for t in range(NT):
                        last = mm(misc[0:3 * NH, P * t:P * (t + 1)], mparts[:, t].rearrange("p n h -> p (n h)"),
                                  identb[:, :], start=True, stop=True)
                elif kind == "heads_out":
                    _, b, g = job
                    pe.wait_ge(heads_read, 2 * b + g + 1)
                    for t in range(NT):
                        last = nc.tensor.transpose(misc[:, P * t:P * (t + 1)], headsT[g][:, P * t:P * (t + 1)], ident[:, :])
                elif kind == "attn_turn":
                    done(pe, ("heads_out", job[1], 0))
                    done(pe, ("heads_out", job[1], 1))
                    for t in range(NT):
                        last = nc.tensor.transpose(misc[:, P * t:P * (t + 1)], attn[:, t].rearrange("p g h d -> p (g h d)"),
                                                   ident[:, :])
                elif kind == "attn_proj":
                    done(pe, ("attn_turn", job[1]))
                    for t in range(NT):
                        last = mm(misc[:, P * t:P * (t + 1)], attnT[:, P * t:P * (t + 1)], wp[:, :], start=True, stop=True)
                elif kind == "freq_sum":
                    done(pe, ("freq", job[1]))
                    for f in range(NT):
                        last = mm(misc[:, f:f + 1], prod[:, P * f:P * (f + 1)], ones[:, 0:1], start=True, stop=(f > 0))
                        if f == 0:
                            last = mm(misc[:, 0:1], kf0[:, job[1], :], bqT[:, :], start=False, stop=True)
                elif kind == "ctx_k":
                    pe.wait_ge(s_cw, 48)
                    for b in range(B):
                        last = mm(misc[0:S2, P * b:P * (b + 1)], ctxT[:, b, :], cwk[:, :], start=True, stop=True)
                elif kind == "ctx_vT":
                    last = mm(misc[:, 0:B * S2], cwv[:, :], ctxT[:, :, :].rearrange("p b s -> p (b s)"), start=True, stop=True)
                elif kind == "w_turn":
                    pe.wait_ge(w_made, 1)
                    for i in range(NI):
                        last = nc.tensor.transpose(misc[:, P * i:P * (i + 1)],
                                                   wdq[:, job[1]].rearrange("p k e -> p (k e)")[:, P * i:P * (i + 1)], ident[:, :])
                elif kind == "ctx_kf":
                    done(pe, ("ctx_k",))
                    pe.wait_ge(s_dft, 16)
                    last = mm(misc, ctxk[:, job[1], :], dft[0:S2, 0, :], start=True, stop=True)
                elif kind == "ctx_z":
                    done(pe, ("ctx_kf", job[1]))
                    last = mm(misc, cwqT[:, :], kfT[job[1] % 2][:, :], start=True, stop=True)
                elif kind == "ctx_vo":
                    done(pe, ("ctx_vT",))
                    for b in range(B):
                        last = mm(misc[0:S2, P * b:P * (b + 1)], vT[:, b, :], cwo[:, :], start=True, stop=True)
                elif kind == "inverse":
                    bs = DELAY_GROUPS[job[1]]
                    done(pe, ("freq_sum", bs[-1]))
                    pe.wait_ge(s_idft, 16)
                    for f in range(NT):
                        last = mm(misc[0:len(bs), :], spec[:, f, bs[0]:bs[-1] + 1], idft[:, f, :], start=(f == 0), stop=(f == NT - 1))
                last.then_inc(misc_filled, 1)

            def waits_for_bank(n):
                m = last_on(BANK[n], n)
                if m is None:
                    return
                if MISC[m][0] == "q":
                    pe.wait_ge(q_rest, MISC[m][1] + 1)
                elif MISC[m][0] == "k":
                    pe.wait_ge(k_rest, MISC[m][1] + 1)
                else:
                    pe.wait_ge(misc_free[BANK[n]], free_count(m))

            pe.wait_ge(warm_made, 1)
            warm_up(5, 8)
            pe.wait_ge(s_const, 2)
            for job in FIRST_JOBS:
                side(job)
            warm_up(5, 28)
            for i in range(NMAX):
                max_unit(0, i)
                if i % 2 == 0:
                    side(BESIDE_JOBS[i // 2])
            side(("max_rows", 0))
            for job in LATE_JOBS:
                side(job)
            for n in range(AHEAD):
                score_unit(n)
            for b in range(B):
                for u in range(UNITS):
                    n = b * UNITS + u
                    if n + AHEAD < ALL_UNITS:
                        score_unit(n + AHEAD)
                    for job in side_jobs(n):
                        if job[0] != "freq":
                            side(job)
                    if b >= 1 and u in FREQ_TILES:
                        freq(("freq", b - 1), FREQ_TILES[u])
                    for i in max_units(b, u):
                        max_unit(b + 1, i)
                    if n >= LAG and (n - LAG) % STEP == STEP - 1:
                        value_step((n - LAG) // STEP)
            value_step(ALL_UNITS // STEP - 1)
            for job in TAIL_JOBS:
                if job[0] == "freq":
                    freq(job, range(NT))
                else:
                    side(job)
            for b in range(B):
                pe.wait_ge(shift_landed[b], 16)
                for t in range(NT):
                    last = mm(ps[:, b, P * t:P * (t + 1)], shift[b][:, P * t:P * (t + 1)], vo[:, b, :],
                              start=True, stop=True)
                last.then_inc(agg_filled, 1)
            for b in range(B):
                pe.wait_ge(x2_made, b + 1)
                for t in range(NT):
                    last = nc.tensor.transpose(ps[:, [4, 5, 6, 0][b], P * t:P * (t + 1)], x2[:, b, t, :], ident[:, :])
                last.then_inc(x2T_filled, 1)

            def turn_max(n):
                pe.wait_ge(max_col, n + 1)
                a = amax1[:, :]
                mm(misc[:, 0:P], bass.AP(tensor=a.tensor, offset=a.offset, ap=[a.ap[0], [0, P]]), ident[:, :],
                   start=True, stop=True).then_inc(max_row, 1)

            turn_max(0)
            warm_up(1, 9)
            for k in range(2 * B * NI):
                kk = k % (B * NI)
                if kk % NI == 0:
                    pe.wait_ge(xq_made, kk // NI + 1)
                if k == 0:
                    pe.wait_ge(x2T_read, B)
                if k >= 6:
                    pe.wait_ge(h_out, k - 5)
                mm(ps[:, k % 6, :], wT[:, k // (B * NI), kk % NI, :], xq[:, kk // NI, :], start=True, stop=True)\
                    .then_inc(h_filled, 1)
                if k == B * NI + 3:
                    turn_max(1)
            for n in range(2, 5):
                turn_max(n)
            pe.wait_ge(h_out, 2 * B * NI)
            warm_up(5, 10)
            for b in range(B):
                pe.wait_ge(oq_made, b + 1)
                for t in range(NT):
                    for i in range(NI):
                        last = mm(ps[:, b, P * t:P * (t + 1)], up[:, b, i * T + P * t:i * T + P * (t + 1)], wT[:, 2, i, :],
                                  start=(i == 0), stop=(i == NI - 1))
                last.then_inc(down_filled, 1)


def tables():
    f = np.concatenate([np.arange(T // 2 + 1), np.arange(1, T // 2)])
    angle = 2 * np.pi * ((f[None, :] * np.arange(T)[:, None]) % T) / T
    cosines = np.arange(T) <= T // 2
    forward = np.where(cosines[None, :], np.cos(angle), np.sin(angle))
    twice = np.where((f == 0) | (f == T // 2), 1.0, 2.0)
    inverse = (forward * twice[None, :] / T / C).T
    parts = np.array([[n != 0, n == 2] for _ in range(D) for n in K_PART])
    return forward.astype(np.float32), np.ascontiguousarray(inverse.astype(np.float32)), parts.astype(np.float32)


def kernel(x, ctx_1024, L0_attn_Wk, L0_attn_Wv, L0_attn_Wq, L0_attn_Wp, L0_attn_bp, L0_xattn_Wq, L0_xattn_bq, L0_xattn_Wk,
           L0_xattn_bk, L0_xattn_Wv, L0_xattn_bv, L0_xattn_Wo, L0_xattn_bo, L0_ffn_w_gate, L0_ffn_w_up, L0_ffn_w_down):
    import concourse.bacc as bacc
    from concourse.bass_utils import run_bass_kernel_spmd

    dft, idft, parts = tables()
    def cat(*arrays):
        return np.concatenate([np.asarray(a) for a in arrays], axis=1)

    def by_rows(w):
        return np.asarray(w).reshape(NI, P, C).transpose(1, 0, 2).reshape(P, NI * C)

    given = {
        "x": x, "xT": np.asarray(x).reshape(B * T, C).T,
        "qkv": cat(np.asarray(L0_attn_Wq).transpose(1, 0, 2).reshape(C, NH * D), L0_attn_Wk, L0_attn_Wv),
        "weights": cat(L0_attn_Wp, np.asarray(L0_xattn_Wq).T, L0_xattn_Wk, L0_xattn_Wv, L0_xattn_Wo),
        "ctxT": np.asarray(ctx_1024).transpose(2, 0, 1),
        "col_bias": np.stack([np.asarray(L0_xattn_bq), np.asarray(L0_xattn_bv)], axis=1),
        "row_bias": np.stack([np.asarray(L0_attn_bp), np.asarray(L0_xattn_bo), np.asarray(L0_xattn_bk)]),
        "ffn": cat(by_rows(L0_ffn_w_gate), by_rows(L0_ffn_w_up), L0_ffn_w_down),
        "dft": dft, "idft": idft, "parts": parts,
    }
    nc = bacc.Bacc("TRN2", target_bir_lowering=False, num_devices=1)
    arrays, args = {}, []
    for name, a in given.items():
        a = np.ascontiguousarray(a)
        arrays[f"in_{name}_dram"] = a
        args.append(nc.dram_tensor(f"in_{name}_dram", a.shape, mybir.dt.from_np(a.dtype), kind="ExternalInput").ap())
    args.append(nc.dram_tensor("out_0_dram", (B, T, C), F32, kind="ExternalOutput").ap())
    decoder_layer(nc, *args)
    r = run_bass_kernel_spmd(nc, [arrays], core_ids=[0])
    return r.results[0]["out_0_dram"]
```

```python
from contextlib import ExitStack

import numpy as np

import concourse.bass as bass
from concourse import mybir

F32 = mybir.dt.float32
BF16 = mybir.dt.bfloat16
I16 = mybir.dt.int16
U16 = mybir.dt.uint16
ALU = mybir.AluOpType
ACT = mybir.ActivationFunctionType
AX = mybir.AxisListType

P = 128
B, T, C = 4, 512, 128
NT = T // P
NH, D = 8, 16
S2 = 77
I = 384
NI = I // P
BLK = 32
NB = C // BLK * NI
TOPK = int(2 * np.log(T))
SCALE = C ** -0.5
EPS = 1e-5
QMAX = 32767.0
MAGIC = 1.5 * 2.0 ** 23
LOWEST = -3.0e38
Q_PART = [0, 0, 0, 1, 1, 2]
K_PART = [0, 1, 2, 0, 1, 0]
NS = D * len(Q_PART)
NM = NS + 3
G = 4
STEP = G
UNITS = 3 * NH
ALL_UNITS = B * UNITS
GROUP = UNITS // 2
AHEAD = 3
LAG = 2
RING = 12

MAX_UNITS = [(t, h, n, P * (t + 1)) for t, n in enumerate((4, 2, 1, 1)) for h in range(0, NH, n)]
NMAX = len(MAX_UNITS)
MAX_SLOTS = 15


def side_jobs(n):
    b, u = divmod(n, UNITS)
    jobs = {
        3: [("heads_out", b - 1, 1)],
        4: [("q", b + 2)],
        6: [("attn_turn", b - 1)],
        8: [("attn_proj", b - 1)],
        9: [("k", b + 2)],
        10: [("v", b + 2)],
        13: [("freq", b - 1)],
        16: [("heads_out", b, 0)],
        17: [("max_rows", b + 1)],
        19: [("freq_sum", b - 1)],
    }.get(u, [])
    if b == B - 1 and u in (9, 10, 11):
        jobs = [("w_turn", u - 9)]
    return [j for j in jobs if 0 <= j[1] < B]


FREQ_TILES = {13: [0], 14: [1], 15: [2, 3]}


def max_units(b, u):
    if b + 1 >= B or u >= MAX_SLOTS:
        return []
    return range(u * NMAX // MAX_SLOTS, (u + 1) * NMAX // MAX_SLOTS)


FIRST_JOBS = [("q", 0), ("k", 0), ("v", 0), ("ctx_k",), ("ctx_vT",)]
BESIDE_JOBS = [("ctx_vo",), ("q", 1), ("ctx_kf", 0), ("k", 1), ("ctx_z", 0), ("v", 1), ("ctx_kf", 1), ("ctx_z", 1)]
LATE_JOBS = [("ctx_kf", 2), ("ctx_kf", 3), ("ctx_z", 2), ("ctx_z", 3)]
START_JOBS = FIRST_JOBS + BESIDE_JOBS + [("max_rows", 0)] + LATE_JOBS
TAIL_JOBS = [("heads_out", B - 1, 1), ("attn_turn", B - 1), ("attn_proj", B - 1), ("inverse", 0), ("freq", B - 1),
             ("freq_sum", B - 1), ("inverse", 1)]
DELAY_GROUPS = [range(B - 1), range(B - 1, B)]
MISC = START_JOBS + [j for n in range(ALL_UNITS) for j in side_jobs(n)] \
    + TAIL_JOBS
ORDER = {j: n for n, j in enumerate(MISC)}
START_BANKS = [6, 7, 0, 1, 2, 5]
BANK = [START_BANKS[n % 6] if n < len(START_JOBS) else 6 + n % 2 for n in range(len(MISC))]


def last_on(bank, before):
    return next((n for n in reversed(range(before)) if BANK[n] == bank), None)


def decoder_layer(nc, x_in, xT_in, qkv_in, weights_in, ctxT_in, col_bias_in, row_bias_in, ffn_in, dft_in, idft_in,
                  parts_in, out):
    with ExitStack() as ctx:
        def sb(name, shape, dt=F32):
            return ctx.enter_context(nc.sbuf_tensor(name, shape, dt))

        def sem(name):
            return ctx.enter_context(nc.semaphore(name))

        W = NI * B * T
        early_q, early_p, early_x = sb("early_q", [P, W]), sb("early_p", [P, W]), sb("early_x", [P, W])
        early_w, early_z = sb("early_w", [P, 3 * 3 * NB * BLK]), sb("early_z", [P, B * T])
        bt = "p (b t) -> p b t"
        probs = early_p[:, :].rearrange("p (i q) -> p i q", i=RING)
        early_xT = sb("early_xT", [P, B * T])
        xT, x2 = early_xT[:, :].rearrange(bt, b=B), early_xT[:, :].rearrange("p (b n c) -> p b n c", b=B, n=NT)
        dft, idft = (early_x[:, i * B * T:(i + 1) * B * T].rearrange("p (n t) -> p n t", n=NT) for i in range(2))
        x = early_x[:, 2 * B * T:W].rearrange("p (b n c) -> p b n c", b=B, n=NT)
        qstack = [early_q[:, i * NH * T // 2:(i + 1) * NH * T // 2].bitcast(BF16).rearrange("p (h t) -> p h t", h=NH)
                  for i in range(3)]
        wdiv, wint, wdq = (early_w[:, i * 3 * NB * BLK:(i + 1) * 3 * NB * BLK]
                           .rearrange("p (w k e) -> p w k e", w=3, k=NB) for i in range(3))
        zT = early_z[:, :].rearrange(bt, b=B)
        gate, up = early_q[:, :].rearrange(bt, b=B), early_p[:, :].rearrange(bt, b=B)
        gate16, sig16 = (early_x[:, i * W // 2:(i + 1) * W // 2].bitcast(d).rearrange(bt, b=B)
                         for i, d in enumerate((I16, U16)))
        up16 = early_w[:, 0:W // 2].bitcast(I16).rearrange(bt, b=B)
        xq = early_z[:, :].rearrange(bt, b=B)
        qkv = sb("qkv", [P, (NH + 2) * D])
        wq, wk, wv = qkv[:, 0:NH * D], qkv[:, NH * D:(NH + 1) * D], qkv[:, (NH + 1) * D:(NH + 2) * D]
        wk6 = sb("wk6", [P, D, len(Q_PART)])
        weights = sb("weights", [P, 5, C])
        wp, cwqT, cwk, cwv, cwo = (weights[:, i] for i in range(5))
        row_bias = sb("row_bias", [P, 3, C])
        bp, bo, bk = (row_bias[:, i] for i in range(3))
        parts = sb("parts", [NS, 2])
        ident, identb = sb("ident", [P, P]), sb("identb", [P, P], BF16)
        maskf, maskb = sb("maskf", [P, P]), sb("maskb", [P, P], BF16)
        ones = sb("ones", [P, P])
        warm = sb("warm", [P, T], BF16)
        qpart = [[sb(f"q{n}_{i}", [P, T], BF16) for n in range(3)] for i in range(2)]
        qrest = [sb(f"qrest{i}", [P, T]) for i in range(2)]
        kstack = [sb(f"kstack{i}", [P, T], BF16) for i in range(3)]
        kfirst, krest = sb("kfirst", [NS, T], BF16), sb("krest", [NS, T])
        ksecond = sb("ksecond", [NS, T], BF16)
        vaug = [sb(f"vaug{i}", [P, NT, 32]) for i in range(3)]
        mneg = sb("mneg", [P, NT, NH])
        mrest = sb("mrest", [P, NT, NH])
        mparts = sb("mparts", [P, NT, 3, NH], BF16)
        mrow = [sb(f"mrow{i}", [3 * NH, T], BF16) for i in range(2)]
        headsT = [sb(f"headsT{g}", [P, T]) for g in range(2)]
        sumr = sb("sumr", [P, NT * 4])
        attn = sb("attn", [P, NT, 2, 4, D])
        attnT = sb("attnT", [P, T])
        z1 = sb("z1", [P, NT, C])
        z2, z3 = (a[:, 0:B * T].rearrange("p (b n c) -> p b n c", b=B, n=NT) for a in (early_q, early_x[:, W // 2:W]))
        stats, mv = sb("stats", [P, NT, 6]), sb("mv", [P, 3 * B, NT, 2])
        veps, half = sb("veps", [P, NT]), sb("half", [P, NT])
        rstd, shiftn = sb("rstd", [P, 3 * B, NT]), sb("shiftn", [P, 3 * B, NT])
        early_1 = sb("early_1", [P, B * T])
        x1, xround = early_1[:, :].rearrange("p (b n c) -> p b n c", b=B, n=NT), early_1[:, :].rearrange(bt, b=B)
        x1b = sb("x1b", [P, B, NT, C])
        ctxT = sb("ctxT", [P, B, S2])
        col_bias = sb("col_bias", [P, 2])
        bq, bv = col_bias[:, 0:1], col_bias[:, 1:2]
        bqT = sb("bqT", [P, 1])
        ctxk = sb("ctxk", [S2, B, C])
        kfT = [sb(f"kfT{i}", [P, T]) for i in range(2)]
        kf0 = sb("kf0", [P, B, P])
        vT = sb("vT", [P, B, S2])
        vo = sb("vo", [S2, B, C])
        prod = sb("prod", [P, T])
        spec = sb("spec", [P, NT, B])
        corr, corr2, corr3, ecorr = (sb(n, [B, T]) for n in ("corr", "corr2", "corr3", "ecorr"))
        top1, top2, sel = sb("top1", [B, 8]), sb("top2", [B, 8]), sb("sel", [B, 8])
        ntop, wsum, wrec = sb("ntop", [B, 1]), sb("wsum", [B, 1]), sb("wrec", [B, 1])
        wts = sb("wts", [B, T])
        wrap = sb("wrap", [B, T + P])
        shift = [sb(f"shift{b}", [S2, T]) for b in range(B)]
        wraw = sb("wraw", [P, 3, NB, BLK])
        wmax, wscl, winv = (sb(n, [P, 3, NB]) for n in ("wmax", "wscl", "winv"))
        wT = sb("wT", [P, 3, NI, P])
        amax = sb("amax", [P, 4, 16])
        amax1 = sb("amax1", [P, 1])
        gmax = sb("gmax", [P, 1])
        scl = sb("scl", [P, 32])
        scrap = sb("scrap", [P, 1])
        signs = [a[:, i * W // B // 2:(i + 1) * W // B // 2].bitcast(BF16)
                 for a in (x1b[:, :, :, :].rearrange("p b n c -> p (b n c)"), early_1) for i in range(2)]
        y3 = early_z[:, :].rearrange("p (b n c) -> p b n c", b=B, n=NT)

        ps = ctx.enter_context(nc.psum_tensor("ps", [P, 8, T], F32))
        heads = ps[:, 5, :]

        NR = len(Q_PART)
        qdram = nc.dram_tensor("q_parts", [B, NH, D, NR, T], BF16, kind="Internal").ap()

        s_x = [sem(f"x_landed{b}") for b in range(B)]
        s_xn = sem("x_nat_landed")
        s_qkv, s_parts, s_bias = sem("qkv_landed"), sem("parts_landed"), sem("bias_landed")
        wk6_made = sem("wk6_made")
        s_cw = sem("ctx_weights_landed")
        s_dft, s_idft = sem("dft_landed"), sem("idft_landed")
        s_wf = sem("ffn_weights_landed")
        s_const = sem("consts_made")
        s_ident = sem("ident_made")
        warm_made = sem("warm_made")
        misc_filled = sem("misc_filled")
        misc_free = [sem(f"misc_free{n}") for n in range(8)]
        q1_made, q_rest, q2_made, q3_made = sem("q1_made"), sem("q_rest"), sem("q2_made"), sem("q3_made")
        q_in_dram, q_landed = sem("q_in_dram"), [sem(f"q_landed{i}") for i in range(3)]
        k1_made, k_rest, k2_made, k_made = sem("k1_made"), sem("k_rest"), sem("k2_made"), sem("k_made")
        smax_filled, smax_read = sem("smax_filled"), sem("smax_read")
        mparts_made = sem("mparts_made")
        m_landed = sem("m_landed")
        scores_filled, exp_done = sem("scores_filled"), sem("exp_done")
        probs_ready, pv_done = sem("probs_ready"), sem("pv_done")
        heads_read = sem("heads_read")
        var_made, rstd_made, x1_made, x1b_made = sem("var_made"), sem("rstd_made"), sem("x1_made"), sem("x1b_made")
        xb_made = sem("xb_made")
        ctx_made = sem("ctx_made")
        w_made = sem("w_made")
        top_made, ecorr_made = sem("top_made"), sem("ecorr_made")
        wrap_made = sem("wrap_made")
        shift_landed = [sem(f"shift_landed{b}") for b in range(B)]
        agg_filled = sem("agg_filled")
        x2_made, x2T_filled, x2T_read, xq_made = sem("x2_made"), sem("x2T_filled"), sem("x2T_read"), sem("xq_made")
        max_col, max_row = sem("max_col"), sem("max_row")
        h_filled, h_out = sem("h_filled"), sem("h_out")
        g16_made, g16_late, gabs_made, sig_made = sem("g16_made"), sem("g16_late"), sem("gabs_made"), sem("sig_made")
        gsign_made, up_maxed, up_signed, osign_made = sem("gsign_made"), sem("up_maxed"), sem("up_signed"), sem("osign_made")
        scales_g, scales_u, scales_h, scales_o = sem("scales_g"), sem("scales_u"), sem("scales_h"), sem("scales_o")
        u16_made, h16_made, o16_made = sem("u16_made"), sem("h16_made"), sem("o16_made")
        oq_made, down_filled = sem("oq_made"), sem("down_filled")
        y_made, y_stored = sem("y_made"), sem("y_stored")
        x2_rest, y_rest = sem("x2_rest"), sem("y_rest")
        pool_ch, dve_ch = sem("pool_chain"), sem("dve_chain")

        block = ctx.enter_context(nc.Block())

        SX, FX, SG, FG, SU, FU, CH, SH, FH, CO, SO, FO, TMP, REC = range(14)

        def col(n):
            return scl[:, n:n + 1]

        def shifted(row):
            a = wrap[row:row + 1, P:P + 1]
            return bass.AP(tensor=a.tensor, offset=a.offset, ap=[a.ap[0], [-1, S2], [1, T]])

        def bank(job):
            return ps[:, BANK[ORDER[job]], :]

        def landed(eng, job):
            eng.wait_ge(misc_filled, ORDER[job] + 1)

        def freed(job):
            return misc_free[BANK[ORDER[job]]]

        def free_count(n):
            return sum(BANK[m] == BANK[n] and MISC[m][0] not in ("q", "k") for m in range(n + 1))

        def done(eng, job):
            eng.wait_ge(freed(job), free_count(ORDER[job]))

        X2T_BANK = (4, 5, 6, 3)
        misc = ps[:, 7, :]

        @block.sync
        def _(sp):
            def bounce(b, between=()):
                for n in range(3):
                    sp.wait_ge((q1_made, q2_made, q3_made)[n], b + 1)
                    r, k = Q_PART.index(n), Q_PART.count(n)
                    a = qpart[b % 2][n][:, :]
                    sp.dma_start(qdram[b, :, :, r:r + k, :].rearrange("h d r q -> (h d) r q"),
                                 bass.AP(tensor=a.tensor, offset=a.offset, ap=[a.ap[0], [0, k], [1, T]]))\
                        .then_inc(q_in_dram, 16)
                    for load in between[n:n + 1]:
                        load()
                sp.wait_ge(q_in_dram, 48 * (b + 1))
                if b >= 3:
                    sp.wait_ge(pv_done, UNITS // STEP * (b - 2))
                sp.dma_start(qstack[b % 3][0:NS, :, :], qdram[b].rearrange("h d r q -> (d r) h q"))\
                    .then_inc(q_landed[b % 3], 16)

            def max_rows(b):
                n = ORDER[("max_rows", b)]
                sp.wait_ge(misc_free[BANK[n]], free_count(n))
                sp.dma_start(qstack[b % 3][NS:NM, :, :], mrow[b % 2][:, :]).then_inc(m_landed, 16)

            def load_ffn():
                sp.dma_start(wraw[:, :, :, :].rearrange("p w k e -> p (w k e)"), ffn_in).then_inc(s_wf, 16)

            def load_bias():
                sp.dma_start(row_bias[:, :, :], bass.AP(tensor=row_bias_in.tensor, offset=row_bias_in.offset,
                                                        ap=[[0, P], [C, 3], [1, C]])).then_inc(s_bias, 16)

            def load_dft():
                sp.dma_start(dft[:, :, :], dft_in.rearrange("(n p) f -> p n f", p=P)).then_inc(s_dft, 16)

            sp.dma_start(xT[:, 0, :], xT_in[:, 0:T]).then_inc(s_x[0], 16)
            sp.dma_start(weights[:, :, :].rearrange("p w c -> p (w c)"), weights_in).then_inc(s_cw, 16)
            sp.dma_start(ctxT[:, :, :], ctxT_in).then_inc(s_cw, 16)
            sp.dma_start(col_bias[:, :], col_bias_in).then_inc(s_cw, 16)
            load_bias()
            bounce(0)
            sp.dma_start(xT[:, 1, :], xT_in[:, T:2 * T]).then_inc(s_x[1], 16)
            load_dft()
            sp.dma_start(x[:, :, :, :], x_in.rearrange("b (n p) c -> p b n c", p=P)).then_inc(s_xn, 16)
            bounce(1)
            for b in range(2, B):
                sp.dma_start(xT[:, b, :], xT_in[:, b * T:(b + 1) * T]).then_inc(s_x[b], 16)
            load_ffn()
            sp.dma_start(idft[:, :, :], idft_in.rearrange("(n p) l -> p n l", p=P)).then_inc(s_idft, 16)
            max_rows(0)
            for b in range(B):
                if b + 2 < B:
                    bounce(b + 2)
                if b + 1 < B:
                    max_rows(b + 1)
            sp.wait_ge(wrap_made, 1)
            for b in (0, 2):
                sp.dma_start(shift[b][:, :], shifted(b)).then_inc(shift_landed[b], 16)
            sp.wait_ge(wrap_made, 2)
            sp.dma_start(shift[B - 1][:, :], shifted(0)).then_inc(shift_landed[B - 1], 16)
            for b in range(B):
                sp.wait_ge(y_made, b + 1)
                if b == B - 1:
                    sp.wait_ge(y_rest, 1)
                sp.dma_start(out[b].rearrange("(n p) c -> p n c", p=P), y3[:, b]).then_inc(y_stored, 16)
            sp.wait_ge(y_stored, 16 * B)

        @block.gpsimd
        def _(pool):
            chain = [0]

            def link(ins):
                chain[0] += 1
                ins.then_inc(pool_ch, 1)
                pool.wait_ge(pool_ch, chain[0])

            g = nc.gpsimd
            g.memset(ones[:, :], 1.0)
            link(g.memset(ident[:, :], 0.0))
            g.affine_select(out=ident[:, :], in_=ident[:, :], compare_op=ALU.not_equal, fill=1.0, base=0,
                            pattern=[[-1, P]], channel_multiplier=1).then_inc(s_ident, 1)
            link(g.memset(maskf[:, :], 0.0))
            link(g.affine_select(out=maskf[:, :], in_=maskf[:, :], compare_op=ALU.is_ge, fill=LOWEST, base=0,
                                 pattern=[[-1, P]], channel_multiplier=1))
            g.tensor_copy(maskb[:, :], maskf[:, :])
            pool.wait_ge(s_ident, 1)
            for i in range(3):
                link(g.memset(vaug[i][:, :, :], 0.0))
                g.memset(vaug[i][:, :, D:D + 1], 1.0)
            g.memset(half[:, :], -0.5)
            g.tensor_copy(identb[:, :], ident[:, :]).then_inc(s_const, 1)

            def q_third(b):
                pool.wait_ge(q2_made, b + 1)
                if b >= 2:
                    pool.wait_ge(q_in_dram, 48 * (b - 1))
                g.tensor_tensor(qpart[b % 2][2][:, :], qrest[b % 2][:, :], qpart[b % 2][1][:, :], ALU.subtract)\
                    .then_inc(q3_made, 1)

            def inv_std(n):
                pool.wait_ge(var_made, n + 1)
                link(g.tensor_scalar(veps[:, :], mv[:, n, :, 1], EPS, None, ALU.add))
                if n < B:
                    g.tensor_tensor(rstd[:, n], veps[:, :], half[:, :], ALU.pow).then_inc(rstd_made, 1)
                    return
                link(g.tensor_tensor(rstd[:, n], veps[:, :], half[:, :], ALU.pow))
                link(g.tensor_tensor(shiftn[:, n], mv[:, n, :, 0], rstd[:, n], ALU.mult))
                g.tensor_scalar(shiftn[:, n], shiftn[:, n], -1.0, None, ALU.mult).then_inc(rstd_made, 1)

            def add_bo(b):
                pool.wait_ge(x1_made, b + 1)
                g.tensor_tensor(x1b[:, b], x1[:, b], bo_b, ALU.add).then_inc(x1b_made, 1)

            bo_b = bass.AP(tensor=bo[:, :].tensor, offset=bo[:, :].offset, ap=[bo[:, :].ap[0], [0, NT], [1, C]])
            bp_b = bass.AP(tensor=bp[:, :].tensor, offset=bp[:, :].offset, ap=[bp[:, :].ap[0], [0, NT], [1, C]])

            def select(i):
                pool.wait_ge(exp_done, STEP * (i + 1))
                pt = probs[:, STEP * i % RING:STEP * i % RING + STEP, :]
                if i % 3 < 2:
                    v, pattern = pt[:, :, 0:P], [[0, STEP], [1, P]]
                else:
                    v = pt.rearrange("p h (j q) -> p h j q", q=2 * P)[:, :, :, 0:P]
                    pattern = [[0, STEP], [0, 2], [1, P]]
                g.affine_select(out=v, in_=v, compare_op=ALU.is_ge, fill=0.0, base=0, pattern=pattern,
                                channel_multiplier=-1).then_inc(probs_ready, 1)

            q_third(0)
            q_third(1)
            pool.wait_ge(s_cw, 48)
            g.tensor_scalar(bqT[:, :], bq[:, :], float(T), None, ALU.mult).then_inc(ctx_made, 1)
            pool.wait_ge(s_bias, 16)
            pool.wait_ge(s_xn, 16)
            for b in range(B):
                g.tensor_tensor(x[:, b], x[:, b], bp_b, ALU.add).then_inc(xb_made, 1)
            for b in range(B):
                for u in range(UNITS):
                    n = b * UNITS + u
                    if n % STEP == 0:
                        select(n // STEP)
                    if u == 8 and b + 2 < B:
                        q_third(b + 2)
                    if u == 9 and b >= 1:
                        inv_std(b - 1)
                    if u == 13 and b >= 1:
                        add_bo(b - 1)
            inv_std(B - 1)
            add_bo(B - 1)
            for n in range(B, 2 * B):
                inv_std(n)
            for k in range(B * NI):
                b, i = divmod(k, NI)
                pool.wait_ge(gsign_made, b + 1)
                pool.wait_ge(up_maxed, k + 1)
                c = slice(i * T, (i + 1) * T)
                g.tensor_tensor(up[:, b, c], up[:, b, c], signs[b][:, c], ALU.mult).then_inc(up_signed, 1)
            for n in range(2 * B, 3 * B):
                inv_std(n)

        @block.scalar
        def _(act):
            s = nc.scalar
            act.dma_start(qkv[:, :], qkv_in).then_inc(s_qkv, 16)
            act.dma_start(parts[:, :], parts_in).then_inc(s_parts, 16)
            act.wait_ge(s_const, 2)
            s.activation(scrap[:, 0:1], half[:, 0:1], ACT.Exp)

            def exps(n):
                act.wait_ge(scores_filled, n + 1)
                if n >= RING:
                    act.wait_ge(pv_done, (n - RING) // STEP + 1)
                w = T if n // STEP % 3 == 0 else T - P
                s.activation(probs[:, n % RING, 0:w], ps[:, n % AHEAD, 0:w], ACT.Exp, scale=SCALE).then_inc(exp_done, 1)

            def heads_evict(k):
                act.wait_ge(pv_done, 3 * (k + 1))
                if k >= 2:
                    act.wait_ge(misc_filled, ORDER[("heads_out", k // 2 - 1, k % 2)] + 1)
                s.activation(headsT[k % 2][:, :], heads, ACT.Copy).then_inc(heads_read, 1)

            def side(job):
                kind = job[0]
                src = bank(job)
                if kind == "q":
                    b = job[1]
                    if b >= 2:
                        act.wait_ge(q_in_dram, 48 * (b - 1))
                    landed(act, job)
                    s.activation(qpart[b % 2][0][:, :], src, ACT.Copy).then_inc(q1_made, 1)
                elif kind == "k":
                    b = job[1]
                    if b >= 1:
                        act.wait_ge(k_rest, b)
                    landed(act, job)
                    s.activation(kfirst[:, :], src[0:NS, :], ACT.Copy).then_inc(k1_made, 1)
                elif kind == "v":
                    b = job[1]
                    landed(act, job)
                    if b >= 3:
                        act.wait_ge(pv_done, UNITS // STEP * (b - 2))
                    s.activation(vaug[b % 3][:, :, 0:D], src[:, 0:NT * D].rearrange("p (n d) -> p n d", n=NT),
                                 ACT.Copy).then_inc(freed(job), 1)
                elif kind == "max_rows":
                    b = job[1]
                    landed(act, job)
                    if b >= 2:
                        act.wait_ge(m_landed, 16 * (b - 1))
                    s.activation(mrow[b % 2][:, :], src[0:3 * NH, :], ACT.Copy).then_inc(freed(job), 1)
                elif kind == "attn_turn":
                    landed(act, job)
                    if job[1] >= 1:
                        act.wait_ge(misc_filled, ORDER[("attn_proj", job[1] - 1)] + 1)
                    s.activation(attnT[:, :], src, ACT.Copy).then_inc(freed(job), 1)
                elif kind == "freq_sum":
                    landed(act, job)
                    s.activation(spec[:, :, job[1]], src[:, 0:NT], ACT.Copy).then_inc(freed(job), 1)
                elif kind == "ctx_vT":
                    landed(act, job)
                    act.wait_ge(s_cw, 48)
                    s.activation(vT[:, :, :], src[:, 0:B * S2].rearrange("p (b s) -> p b s", b=B), ACT.Identity,
                                 bias=bv[:, 0:1]).then_inc(freed(job), 1)
                elif kind == "w_turn":
                    landed(act, job)
                    s.activation(wT[:, job[1]], src[:, 0:NI * P].rearrange("p (i o) -> p i o", i=NI), ACT.Copy)\
                        .then_inc(freed(job), 1)
                elif kind == "ctx_kf":
                    b = job[1]
                    landed(act, job)
                    if b >= 2:
                        act.wait_ge(misc_filled, ORDER[("ctx_z", b - 2)] + 1)
                    s.activation(kf0[:, b, 0:1], src[:, 0:1], ACT.Copy)
                    s.activation(kfT[b % 2][:, :], src, ACT.Copy).then_inc(freed(job), 1)
                elif kind == "ctx_z":
                    landed(act, job)
                    s.activation(zT[:, job[1], :], src, ACT.Copy).then_inc(freed(job), 1)
                elif kind == "ctx_vo":
                    landed(act, job)
                    s.activation(vo[:, :, :], src[0:S2, :].rearrange("p (b c) -> p b c", b=B), ACT.Copy)\
                        .then_inc(freed(job), 1)

            def second_part(job):
                kind, b = job[0], job[1]
                if kind == "q":
                    act.wait_ge(q_rest, b + 1)
                    s.activation(qpart[b % 2][1][:, :], qrest[b % 2][:, :], ACT.Copy).then_inc(q2_made, 1)
                elif kind == "k":
                    act.wait_ge(k_rest, b + 1)
                    if b >= 1:
                        act.wait_ge(k_made, b)
                    s.activation(ksecond[:, :], krest[:, :], ACT.Copy).then_inc(k2_made, 1)

            for n, job in enumerate(START_JOBS):
                side(job)
                if n > 0 and START_JOBS[n - 1][0] in ("q", "k"):
                    second_part(START_JOBS[n - 1])
            for n in range(AHEAD):
                exps(n)
            for b in range(B):
                for u in range(UNITS):
                    n = b * UNITS + u
                    if n + AHEAD < ALL_UNITS:
                        exps(n + AHEAD)
                    if n >= LAG and (n - LAG) % GROUP == GROUP - 1:
                        heads_evict((n - LAG) // GROUP)
                    for job in side_jobs(n - 1):
                        side(job)
                    for job in side_jobs(n - 3):
                        if job[0] in ("q", "k"):
                            second_part(job)
            heads_evict(2 * B - 1)
            def delay_exp(g):
                n = len(DELAY_GROUPS[g])
                act.wait_ge(top_made, g + 1)
                s.activation(ecorr[0:n, :], corr[0:n, :], ACT.Exp, bias=ntop[0:n, 0:1]).then_inc(ecorr_made, 1)

            for job in TAIL_JOBS:
                if job == ("inverse", 0):
                    delay_exp(0)
                else:
                    side(job)
            act.wait_ge(wrap_made, 1)
            act.dma_start(shift[1][:, :], shifted(1)).then_inc(shift_landed[1], 16)
            delay_exp(1)

            def normalise(n, src, dst, made):
                act.wait_ge(rstd_made, n + 1)
                for t in range(NT // 2 if n % B == B - 1 else NT):
                    ins = s.activation(dst[:, n % B, t, :], src[:, n % B, t, :], ACT.Identity,
                                       bias=shiftn[:, n, t:t + 1], scale=rstd[:, n, t:t + 1])
                ins.then_inc(made, 1)

            for b in range(B):
                normalise(B + b, z2, x2, x2_made)
            s.activation(scrap[:, 0:1], half[:, 0:1], ACT.Sigmoid)
            for b in range(B):
                act.wait_ge(x2T_read, b + 1)
                s.activation(xq[:, b], xround[:, b], ACT.Copy, bias=-MAGIC).then_inc(xq_made, 1)

            def hidden_out(k):
                hid = gate if k < B * NI else up
                kk = k % (B * NI)
                act.wait_ge(h_filled, k + 1)
                s.activation(hid[:, kk // NI, (kk % NI) * T:(kk % NI + 1) * T], ps[:, k % 6, :], ACT.Copy).then_inc(h_out, 1)

            def gate_sign(b):
                act.wait_ge(h_out, (b + 1) * NI)
                s.activation(signs[b], gate[:, b], ACT.Sign).then_inc(gsign_made, 1)

            for k in range(B * NI):
                hidden_out(k)
                if k % NI == NI - 1 and k // NI < B - 2:
                    gate_sign(k // NI)
            for k in range(B * NI, (B + 1) * NI):
                hidden_out(k)
            for b in range(B - 2, B):
                gate_sign(b)
            for b in range(B):
                if b == B - 1:
                    s.activation(gate16[:, b], gate[:, b], ACT.Copy, scale=col(FG)).then_inc(g16_late, 1)
                    act.wait_ge(g16_late, 1)
                else:
                    act.wait_ge(g16_made, b + 1)
                act.wait_ge(gsign_made, b + 1)
                s.activation(gate[:, b], gate16[:, b], ACT.Sigmoid, scale=col(SG)).then_inc(sig_made, 1)
                s.activation(gate16[:, b], gate16[:, b], ACT.Abs).then_inc(gabs_made, 1)
                if b < B - 1:
                    for i in range(NI):
                        hidden_out((B + b + 1) * NI + i)
            act.wait_ge(scales_u, 1)
            for b in range(B):
                act.wait_ge(up_signed, (b + 1) * NI)
                s.activation(up16[:, b], up[:, b], ACT.Abs, scale=col(FU)).then_inc(u16_made, 1)
            for b in range(2):
                s.activation(signs[b], up[:, b], ACT.Sign).then_inc(osign_made, 1)
            act.wait_ge(scales_h, 1)
            for b in range(2, B):
                s.activation(gate16[:, b], gate[:, b], ACT.Copy, scale=col(FH)).then_inc(h16_made, 1)
            for b in range(2, B):
                s.activation(signs[b], up[:, b], ACT.Sign).then_inc(osign_made, 1)
            act.wait_ge(scales_o, 1)
            for b in range(1, B):
                s.activation(gate16[:, b], gate[:, b], ACT.Copy, scale=col(FO)).then_inc(o16_made, 1)
            for b in range(B):
                normalise(2 * B + b, z3, y3, y_made)

        @block.vector
        def _(dve):
            v = nc.vector
            chain = [0]

            def link(ins):
                chain[0] += 1
                ins.then_inc(dve_ch, 1)
                dve.wait_ge(dve_ch, chain[0])

            def max_unit(b, i):
                t, h, n, w = MAX_UNITS[i]
                m = NMAX * b + i
                dve.wait_ge(smax_filled, m + 1)
                v.tensor_reduce(mneg[:, t, h:h + n], ps[:, 3 + m % 2, 0:n * w].rearrange("p (h s) -> p h s", h=n),
                                AX.X, ALU.max, negate=True).then_inc(smax_read, 1)
                if i == NMAX - 1:
                    if b >= 1:
                        dve.wait_ge(misc_filled, ORDER[("max_rows", b - 1)] + 1)
                    dve.wait_ge(smax_read, NMAX * (b + 1))
                    link(v.tensor_copy(mparts[:, :, 0, :], mneg[:, :, :]))
                    link(v.tensor_tensor(mrest[:, :, :], mneg[:, :, :], mparts[:, :, 0, :], ALU.subtract))
                    link(v.tensor_copy(mparts[:, :, 1, :], mrest[:, :, :]))
                    v.tensor_tensor(mparts[:, :, 2, :], mrest[:, :, :], mparts[:, :, 1, :], ALU.subtract)\
                        .then_inc(mparts_made, 1)

            def norm_stats(n, z):
                for t in range(NT):
                    ins = v.bn_stats(stats[:, t, :], z[:, t, :])
                link(ins)
                for t in range(NT):
                    ins = v.bn_aggr(mv[:, n, t, :], stats[:, t, :])
                ins.then_inc(var_made, 1)

            def normalise(n, z, dst, tiles=range(NT)):
                dve.wait_ge(rstd_made, n + 1)
                dve.wait_ge(var_made, n + 1)
                for t in tiles:
                    ins = v.tensor_scalar(dst[:, t, :], z[:, t, :], mv[:, n, t, 0:1], rstd[:, n, t:t + 1],
                                          ALU.subtract, ALU.mult)
                return ins

            bk_b = bass.AP(tensor=bk[:, :].tensor, offset=bk[0:S2, :].offset, ap=[bk[0:S2, :].ap[0], [0, B], [1, C]])

            def side(job):
                kind = job[0]
                src = bank(job)
                if kind == "q":
                    b = job[1]
                    if b >= 2:
                        dve.wait_ge(q3_made, b - 1)
                    dve.wait_ge(q1_made, b + 1)
                    v.tensor_tensor(qrest[b % 2][:, :], src, qpart[b % 2][0][:, :], ALU.subtract).then_inc(q_rest, 1)
                elif kind == "k":
                    b = job[1]
                    if b >= 1:
                        dve.wait_ge(k2_made, b)
                        dve.wait_ge(k_made, b)
                    dve.wait_ge(k1_made, b + 1)
                    v.scalar_tensor_tensor(krest[:, :], kfirst[:, :], parts[:, 0:1], src[0:NS, :],
                                           ALU.mult, ALU.subtract).then_inc(k_rest, 1)
                elif kind == "heads_out":
                    _, b, g = job
                    landed(dve, job)
                    if g == 0 and b >= 1:
                        dve.wait_ge(misc_filled, ORDER[("attn_turn", b - 1)] + 1)
                    link(v.reciprocal(sumr[:, :], src.rearrange("p (k e) -> p k e", e=32)[:, :, D]))
                    rec = sumr[:, :]
                    rec = bass.AP(tensor=rec.tensor, offset=rec.offset, ap=[rec.ap[0], [4, NT], [1, 4], [0, D]])
                    v.tensor_tensor(attn[:, :, g], src.rearrange("p (t h e) -> p t h e", t=NT, h=4)[:, :, :, 0:D], rec,
                                    ALU.mult).then_inc(freed(job), 1)
                elif kind == "attn_proj":
                    b = job[1]
                    landed(dve, job)
                    dve.wait_ge(xb_made, b + 1)
                    dve.wait_ge(x1_made, b)
                    v.tensor_tensor(z1[:, :, :], src.rearrange("p (t c) -> p t c", t=NT), x[:, b], ALU.add)\
                        .then_inc(freed(job), 1)
                    dve.wait_ge(freed(job), free_count(ORDER[job]))
                    norm_stats(b, z1)
                elif kind == "freq":
                    b = job[1]
                    landed(dve, job)
                    if b >= 1:
                        dve.wait_ge(misc_filled, ORDER[("freq_sum", b - 1)] + 1)
                    v.tensor_tensor(prod[:, :], src, zT[:, b, :], ALU.mult).then_inc(freed(job), 1)
                elif kind == "ctx_k":
                    landed(dve, job)
                    dve.wait_ge(s_bias, 16)
                    v.tensor_tensor(ctxk[:, :, :], src[0:S2, :].rearrange("p (b c) -> p b c", b=B), bk_b, ALU.add)\
                        .then_inc(freed(job), 1)

            def k_last(b):
                dve.wait_ge(k2_made, b + 1)
                if b >= 3:
                    dve.wait_ge(pv_done, UNITS // STEP * (b - 2))
                v.scalar_tensor_tensor(kstack[b % 3][0:NS, :], ksecond[:, :], parts[:, 1:2], krest[:, :],
                                       ALU.mult, ALU.subtract).then_inc(k_made, 1)

            v.memset(warm[:, :], 1.0).then_inc(warm_made, 1)
            dve.wait_ge(s_qkv, 16)
            a = wk[:, :]
            v.tensor_copy(wk6[:, :, :], bass.AP(tensor=a.tensor, offset=a.offset, ap=[a.ap[0], [1, D], [0, NR]]))\
                .then_inc(wk6_made, 1)
            ins = v.memset(kf0[:, :, :], 0.0)
            ins.then_inc(s_const, 1)
            for i in range(3):
                v.memset(kstack[i][NS:NS + 32, :], 1.0)
            dve.wait_ge(s_parts, 16)
            for job in FIRST_JOBS:
                side(job)
                if job[0] == "k":
                    k_last(job[1])
            def round_weights():
                dve.wait_ge(s_wf, 16)
                w3 = wraw[:, :, :, :].rearrange("p w k e -> p (w k) e")
                link(v.tensor_reduce(wmax[:, :, :].rearrange("p w k -> p (w k)"), w3, AX.X, ALU.max, apply_absolute_value=True))
                link(v.tensor_scalar(wscl[:, :, :], wmax[:, :, :], 1.0 / 7.0, 1e-12, ALU.mult, ALU.max))
                link(v.reciprocal(winv[:, :, :], wscl[:, :, :]))
                sw, iw = (bass.AP(tensor=a.tensor, offset=a.offset, ap=[a.ap[0], [1, 3 * NB], [0, BLK]])
                          for a in (wscl[:, :, :], winv[:, :, :]))
                flat = "p w k e -> p (w k) e"
                link(v.tensor_tensor(wdiv[:, :, :, :].rearrange(flat), w3, iw, ALU.mult))
                link(v.tensor_scalar(wint[:, :, :, :], wdiv[:, :, :, :], MAGIC, MAGIC, ALU.add, ALU.subtract))
                link(v.tensor_scalar(wdiv[:, :, :, :], wint[:, :, :, :], -8.0, 7.0, ALU.max, ALU.min))
                v.tensor_tensor(wdq[:, :, :, :].rearrange(flat), wdiv[:, :, :, :].rearrange(flat), sw, ALU.mult)\
                    .then_inc(w_made, 1)

            for i in range(NMAX):
                max_unit(0, i)
                if i < 2 or i // 2 > len(BESIDE_JOBS):
                    continue
                job = BESIDE_JOBS[i // 2 - 1]
                if i % 2 == 0 and job[0] in ("q", "k"):
                    side(job)
                if i % 2 == 1 and job[0] == "k":
                    k_last(job[1])
            for b in range(B):
                for u in range(UNITS):
                    n = b * UNITS + u
                    for i in max_units(b, u):
                        max_unit(b + 1, i)
                    for job in side_jobs(n - 1):
                        if job[0] in ("heads_out", "attn_proj"):
                            side(job)
                    for job in side_jobs(n - 2):
                        if job[0] in ("q", "k"):
                            side(job)
                    if u == 16 and b >= 1:
                        side(("freq", b - 1))
                    if u == 13 and b + 2 < B:
                        k_last(b + 2)
                    if b == B - 2 and u == 19:
                        round_weights()
                    if b >= 1 and u == 11:
                        normalise(b - 1, z1, x1[:, b - 1]).then_inc(x1_made, 1)
            for job in TAIL_JOBS[:3]:
                side(job)
            normalise(B - 1, z1, x1[:, B - 1]).then_inc(x1_made, 1)

            def largest_delays(g):
                n = len(DELAY_GROUPS[g])
                landed(dve, ("inverse", g))
                v.tensor_copy(corr[0:n, :], bank(("inverse", g))[0:n, :]).then_inc(freed(("inverse", g)), 1)
                done(dve, ("inverse", g))
                link(v.max(top1[0:n, :], corr[0:n, :]))
                v.tensor_scalar(ntop[0:n, :], top1[0:n, 0:1], -1.0, None, ALU.mult).then_inc(top_made, 1)
                link(v.match_replace(corr2[0:n, :], top1[0:n, :], corr[0:n, :], LOWEST))
                link(v.max(top2[0:n, :], corr2[0:n, :]))

            def delay_weights(g):
                n = len(DELAY_GROUPS[g])
                v.tensor_copy(sel[0:n, 0:TOPK - 8], top2[0:n, 0:TOPK - 8])
                link(v.memset(sel[0:n, TOPK - 8:8], LOWEST))
                link(v.match_replace(corr3[0:n, :], sel[0:n, :], corr2[0:n, :], LOWEST))
                dve.wait_ge(ecorr_made, g + 1)
                link(v.scalar_tensor_tensor(wts[0:n, :], corr3[0:n, :], LOWEST, ecorr[0:n, :], ALU.is_equal, ALU.mult,
                                            accum_out=wsum[0:n, :]))
                link(v.reciprocal(wrec[0:n, :], wsum[0:n, :]))
                if g > 0:
                    for b in DELAY_GROUPS[g - 1]:
                        dve.wait_ge(shift_landed[b], 16)
                a = wts[0:n, :]
                back = bass.AP(tensor=a.tensor, offset=a.offset + T - 1, ap=[a.ap[0], [-1, T - 1]])
                v.tensor_scalar(wrap[0:n, P + 1:P + T], back, wrec[0:n, 0:1], None, ALU.mult)
                v.tensor_scalar(wrap[0:n, P:P + 1], wts[0:n, 0:1], wrec[0:n, 0:1], None, ALU.mult)
                back = bass.AP(tensor=a.tensor, offset=a.offset + P, ap=[a.ap[0], [-1, P]])
                v.tensor_scalar(wrap[0:n, 0:P], back, wrec[0:n, 0:1], None, ALU.mult).then_inc(wrap_made, 1)

            largest_delays(0)
            side(("freq", B - 1))
            delay_weights(0)
            largest_delays(1)
            delay_weights(1)

            def largest_x2(b):
                dve.wait_ge(x2_made, b + 1)
                return v.tensor_reduce(amax[:, 0, b:b + 1], x2[:, b].rearrange("p t c -> p (t c)"), AX.X, ALU.max,
                                       apply_absolute_value=True)

            for b in range(B):
                dve.wait_ge(agg_filled, b + 1)
                dve.wait_ge(x1b_made, b + 1)
                link(v.tensor_tensor(z2[:, b], ps[:, b, :].rearrange("p (t c) -> p t c", t=NT), x1b[:, b], ALU.add))
                norm_stats(B + b, z2[:, b])
                if b >= 2:
                    largest_x2(b - 2)
            largest_x2(B - 2)
            normalise(2 * B - 1, z2[:, B - 1], x2[:, B - 1], range(NT // 2, NT)).then_inc(x2_rest, 1)
            dve.wait_ge(x2_rest, 1)
            link(largest_x2(B - 1))

            def column(row, count):
                v.tensor_reduce(amax1[:, :], amax[:, row, 0:count], AX.X, ALU.max).then_inc(max_col, 1)

            def largest(n):
                dve.wait_ge(max_row, n + 1)
                link(v.tensor_reduce(gmax[:, :], misc[:, 0:P], AX.X, ALU.max))

            def scale_of(c, s_out, f_out, ready=None):
                link(v.tensor_scalar(col(s_out), gmax[:, :], 1.0 / QMAX if c is None else col(TMP), 1e-12, ALU.mult, ALU.max))
                ins = v.reciprocal(col(f_out if c is None else REC), col(s_out))
                if c is not None:
                    link(ins)
                    ins = v.tensor_tensor(col(f_out), col(REC), col(c), ALU.mult)
                if ready is None:
                    link(ins)
                else:
                    ins.then_inc(ready, 1)
                    dve.wait_ge(ready, 1)

            def over_qmax(c):
                link(v.tensor_scalar(col(TMP), col(c), 1.0 / QMAX, None, ALU.mult))

            column(0, B)
            largest(0)
            scale_of(None, SX, FX)
            for b in range(B):
                dve.wait_ge(x2T_filled, b + 1)
                v.tensor_scalar(xround[:, b], ps[:, X2T_BANK[b], :], col(FX), MAGIC, ALU.mult, ALU.add)\
                    .then_inc(x2T_read, 1)
            over_qmax(SX)

            def hidden_max(hid, row, k):
                kk = k % (B * NI)
                dve.wait_ge(h_out, k + 1)
                return v.tensor_reduce(amax[:, row, kk:kk + 1], hid[:, kk // NI, (kk % NI) * T:(kk % NI + 1) * T], AX.X, ALU.max,
                                       apply_absolute_value=True)

            def product(b, a16, b16, row):
                link(v.tensor_tensor_reduce(gate[:, b], a16[:, b], b16[:, b], 1.0, 0.0, ALU.mult, ALU.max,
                                            accum_out=amax[:, row, b:b + 1]))

            for k in range(B * NI):
                last = hidden_max(gate, 0, k)
            link(last)
            column(0, B * NI)
            hidden_max(up, 1, B * NI).then_inc(up_maxed, 1)
            largest(1)
            scale_of(SX, SG, FG, scales_g)
            for b in range(B - 1):
                v.tensor_scalar(gate16[:, b], gate[:, b], col(FG), None, ALU.mult).then_inc(g16_made, 1)
            link(v.tensor_scalar(col(CH), col(SG), 1.0 / 65536.0, None, ALU.mult))
            for b in range(B):
                for i in range(b == 0, NI):
                    hidden_max(up, 1, (B + b) * NI + i).then_inc(up_maxed, 1)
                if b == B - 1:
                    dve.wait_ge(up_maxed, B * NI)
                    column(1, B * NI)
                dve.wait_ge(sig_made, b + 1)
                link(v.tensor_scalar(sig16[:, b], gate[:, b], 65536.0, 65535.0, ALU.mult, ALU.min))
                if b == B - 1:
                    largest(2)
                    scale_of(SX, SU, FU, scales_u)
                dve.wait_ge(gabs_made, b + 1)
                product(b, gate16, sig16, 2)
            column(2, B)
            over_qmax(CH)
            largest(3)
            scale_of(CH, SH, FH, scales_h)
            link(v.tensor_tensor(col(CO), col(SH), col(SU), ALU.mult))
            for b in range(B):
                if b < 2:
                    link(v.tensor_scalar(gate16[:, b], gate[:, b], col(FH), None, ALU.mult))
                else:
                    dve.wait_ge(h16_made, b - 1)
                dve.wait_ge(u16_made, b + 1)
                product(b, gate16, up16, 0)
            column(0, B)
            over_qmax(CO)
            largest(4)
            scale_of(CO, SO, FO, scales_o)

            def signed(b):
                if b == 0:
                    link(v.tensor_scalar(gate16[:, b], gate[:, b], col(FO), None, ALU.mult))
                else:
                    dve.wait_ge(o16_made, b)
                dve.wait_ge(osign_made, b + 1)
                v.tensor_tensor(up[:, b], gate16[:, b], signs[b], ALU.mult).then_inc(oq_made, 1)

            def third_norm(b):
                dve.wait_ge(down_filled, b + 1)
                link(v.scalar_tensor_tensor(z3[:, b].rearrange("p t c -> p (t c)"), ps[:, b, :], col(SO),
                                            x2[:, b].rearrange("p t c -> p (t c)"), ALU.mult, ALU.add))
                norm_stats(2 * B + b, z3[:, b])

            for b in range(B + 1):
                if b < B:
                    signed(b)
                if b >= 2:
                    third_norm(b - 2)
            third_norm(B - 1)
            normalise(3 * B - 1, z3[:, B - 1], y3[:, B - 1], range(NT // 2, NT)).then_inc(y_rest, 1)

        @block.tensor
        def _(pe):
            mm = nc.tensor.matmul

            def warm_up(bank, count):
                for _ in range(count):
                    mm(ps[:, bank, :], warm[:, 0:P], warm[:, :], start=True, stop=True)

            def score_unit(n):
                b, u = divmod(n, UNITS)
                i, hh = divmod(u, STEP)
                h, kind = i // 3 * G + hh, i % 3
                if n >= AHEAD:
                    pe.wait_ge(exp_done, n - AHEAD + 1)
                else:
                    m = last_on(n, len(START_JOBS))
                    pe.wait_ge(misc_free[n], free_count(m))
                if u == 0:
                    warm_up(n % AHEAD, 6)
                    pe.wait_ge(m_landed, 16 * (b + 1))
                q, k, sc = qstack[b % 3], kstack[b % 3], ps[:, n % AHEAD, :]
                if kind < 2:
                    last = mm(sc[:, 0:T - P * kind], k[0:NM, P * kind:P * (kind + 1)], q[0:NM, h, P * kind:T],
                              start=True, stop=True)
                else:
                    mm(sc[:, 0:2 * P], k[0:NM, 2 * P:3 * P], q[0:NM, h, 2 * P:T], start=True, stop=True)
                    last = mm(sc[:, 2 * P:3 * P], k[0:NM, 3 * P:T], q[0:NM, h, 3 * P:T], start=True, stop=True)
                last.then_inc(scores_filled, 1)

            def value_step(i):
                b, kind = i // (UNITS // STEP), i % 3
                pe.wait_ge(probs_ready, i + 1)
                if i == 0:
                    pe.wait_ge(misc_free[5], free_count(last_on(5, len(START_JOBS))))
                elif kind == 0:
                    pe.wait_ge(heads_read, i // 3)
                if i % (UNITS // STEP) == 0:
                    done(pe, ("v", b))
                va = vaug[b % 3]
                for j in ((0,), (1,), (2, 3))[kind]:
                    for hh in range(G):
                        pt = probs[:, (STEP * i + hh) % RING, :]
                        pt = pt[:, 2 * P:3 * P] if j == 3 else pt[:, 0:T - P * j]
                        last = mm(heads[32 * hh:32 * hh + 32, P * j:T], va[:, j, :], pt, start=(j == 0), stop=(j == 3))
                last.then_inc(pv_done, 1)

            def max_unit(b, i):
                t, h0, n, w = MAX_UNITS[i]
                if i == 0:
                    pe.wait_ge(q_landed[b % 3], 16 * (b // 3 + 1))
                    pe.wait_ge(k_made, b + 1)
                m = NMAX * b + i
                if m >= 2:
                    pe.wait_ge(smax_read, m - 1)
                if b == 0 and i >= 2 * len(BESIDE_JOBS):
                    warm_up(3 + m % 2, 1)
                for h in range(n):
                    o = ps[:, 3 + m % 2, h * w:(h + 1) * w]
                    mm(o, qstack[b % 3][0:NS, h0 + h, P * t:P * (t + 1)], kstack[b % 3][0:NS, 0:w], start=True, stop=False)
                    last = mm(o[:, w - P:w], identb[:, :], maskb[:, :], start=False, stop=True)
                last.then_inc(smax_filled, 1)

            def freq(job, tiles):
                if tiles[0] == 0:
                    waits_for_bank(ORDER[job])
                    pe.wait_ge(x1_made, job[1] + 1)
                for t in tiles:
                    last = mm(bank(job), x1[:, job[1], t, :], dft[:, t, :], start=(t == 0), stop=(t == NT - 1))
                if t == NT - 1:
                    last.then_inc(misc_filled, 1)

            def side(job):
                n, kind = ORDER[job], job[0]
                misc = bank(job)
                waits_for_bank(n)
                if kind == "q":
                    pe.wait_ge(s_qkv, 16)
                    pe.wait_ge(s_x[job[1]], 16)
                    last = mm(misc, wq[:, :], xT[:, job[1], :], start=True, stop=True)
                elif kind == "k":
                    pe.wait_ge(wk6_made, 1)
                    last = mm(misc[0:NS, :], wk6[:, :, :].rearrange("p d r -> p (d r)"), xT[:, job[1], :],
                              start=True, stop=True)
                elif kind == "v":
                    pe.wait_ge(s_qkv, 16)
                    for t in range(NT):
                        last = mm(misc[:, t * D:(t + 1) * D], xT[:, job[1], P * t:P * (t + 1)], wv[:, :],
                                  start=True, stop=True)
                elif kind == "max_rows":
                    pe.wait_ge(mparts_made, job[1] + 1)
                    for t in range(NT):
                        last = mm(misc[0:3 * NH, P * t:P * (t + 1)], mparts[:, t].rearrange("p n h -> p (n h)"),
                                  identb[:, :], start=True, stop=True)
                elif kind == "heads_out":
                    _, b, g = job
                    pe.wait_ge(heads_read, 2 * b + g + 1)
                    for t in range(NT):
                        last = nc.tensor.transpose(misc[:, P * t:P * (t + 1)], headsT[g][:, P * t:P * (t + 1)], ident[:, :])
                elif kind == "attn_turn":
                    done(pe, ("heads_out", job[1], 0))
                    done(pe, ("heads_out", job[1], 1))
                    for t in range(NT):
                        last = nc.tensor.transpose(misc[:, P * t:P * (t + 1)], attn[:, t].rearrange("p g h d -> p (g h d)"),
                                                   ident[:, :])
                elif kind == "attn_proj":
                    done(pe, ("attn_turn", job[1]))
                    for t in range(NT):
                        last = mm(misc[:, P * t:P * (t + 1)], attnT[:, P * t:P * (t + 1)], wp[:, :], start=True, stop=True)
                elif kind == "freq_sum":
                    done(pe, ("freq", job[1]))
                    for f in range(NT):
                        last = mm(misc[:, f:f + 1], prod[:, P * f:P * (f + 1)], ones[:, 0:1], start=True, stop=(f > 0))
                        if f == 0:
                            last = mm(misc[:, 0:1], kf0[:, job[1], :], bqT[:, :], start=False, stop=True)
                elif kind == "ctx_k":
                    pe.wait_ge(s_cw, 48)
                    for b in range(B):
                        last = mm(misc[0:S2, P * b:P * (b + 1)], ctxT[:, b, :], cwk[:, :], start=True, stop=True)
                elif kind == "ctx_vT":
                    last = mm(misc[:, 0:B * S2], cwv[:, :], ctxT[:, :, :].rearrange("p b s -> p (b s)"), start=True, stop=True)
                elif kind == "w_turn":
                    pe.wait_ge(w_made, 1)
                    for i in range(NI):
                        last = nc.tensor.transpose(misc[:, P * i:P * (i + 1)],
                                                   wdq[:, job[1]].rearrange("p k e -> p (k e)")[:, P * i:P * (i + 1)], ident[:, :])
                elif kind == "ctx_kf":
                    done(pe, ("ctx_k",))
                    pe.wait_ge(s_dft, 16)
                    last = mm(misc, ctxk[:, job[1], :], dft[0:S2, 0, :], start=True, stop=True)
                elif kind == "ctx_z":
                    done(pe, ("ctx_kf", job[1]))
                    last = mm(misc, cwqT[:, :], kfT[job[1] % 2][:, :], start=True, stop=True)
                elif kind == "ctx_vo":
                    done(pe, ("ctx_vT",))
                    for b in range(B):
                        last = mm(misc[0:S2, P * b:P * (b + 1)], vT[:, b, :], cwo[:, :], start=True, stop=True)
                elif kind == "inverse":
                    bs = DELAY_GROUPS[job[1]]
                    done(pe, ("freq_sum", bs[-1]))
                    pe.wait_ge(s_idft, 16)
                    for f in range(NT):
                        last = mm(misc[0:len(bs), :], spec[:, f, bs[0]:bs[-1] + 1], idft[:, f, :], start=(f == 0), stop=(f == NT - 1))
                last.then_inc(misc_filled, 1)

            def waits_for_bank(n):
                m = last_on(BANK[n], n)
                if m is None:
                    return
                if MISC[m][0] == "q":
                    pe.wait_ge(q_rest, MISC[m][1] + 1)
                elif MISC[m][0] == "k":
                    pe.wait_ge(k_rest, MISC[m][1] + 1)
                else:
                    pe.wait_ge(misc_free[BANK[n]], free_count(m))

            pe.wait_ge(warm_made, 1)
            warm_up(5, 8)
            pe.wait_ge(s_const, 2)
            for job in FIRST_JOBS:
                side(job)
            warm_up(5, 16)
            for i in range(NMAX):
                max_unit(0, i)
                if i % 2 == 0 and i // 2 < len(BESIDE_JOBS):
                    side(BESIDE_JOBS[i // 2])
            side(("max_rows", 0))
            for job in LATE_JOBS:
                side(job)
            for n in range(AHEAD):
                score_unit(n)
            for b in range(B):
                for u in range(UNITS):
                    n = b * UNITS + u
                    if n + AHEAD < ALL_UNITS:
                        score_unit(n + AHEAD)
                    for job in side_jobs(n):
                        if job[0] != "freq":
                            side(job)
                    if b >= 1 and u in FREQ_TILES:
                        freq(("freq", b - 1), FREQ_TILES[u])
                    for i in max_units(b, u):
                        max_unit(b + 1, i)
                    if n >= LAG and (n - LAG) % STEP == STEP - 1:
                        value_step((n - LAG) // STEP)
            value_step(ALL_UNITS // STEP - 1)
            for job in TAIL_JOBS:
                if job[0] == "freq":
                    freq(job, range(NT))
                else:
                    side(job)
            for b in range(B):
                pe.wait_ge(shift_landed[b], 16)
                for t in range(NT):
                    last = mm(ps[:, b, P * t:P * (t + 1)], shift[b][:, P * t:P * (t + 1)], vo[:, b, :],
                              start=True, stop=True)
                last.then_inc(agg_filled, 1)
            def x2_turn(b):
                pe.wait_ge(x2_made, b + 1)
                if b == B - 1:
                    pe.wait_ge(x2_rest, 1)
                for t in range(NT):
                    last = nc.tensor.transpose(ps[:, X2T_BANK[b], P * t:P * (t + 1)], x2[:, b, t, :], ident[:, :])
                last.then_inc(x2T_filled, 1)

            def turn_max(n):
                pe.wait_ge(max_col, n + 1)
                a = amax1[:, :]
                mm(misc[:, 0:P], bass.AP(tensor=a.tensor, offset=a.offset, ap=[a.ap[0], [0, P]]), ident[:, :],
                   start=True, stop=True).then_inc(max_row, 1)

            for b in range(B - 1):
                x2_turn(b)
            turn_max(0)
            x2_turn(B - 1)
            warm_up(1, 3)
            for k in range(2 * B * NI):
                kk = k % (B * NI)
                if kk % NI == 0:
                    pe.wait_ge(xq_made, kk // NI + 1)
                if k == X2T_BANK[B - 1]:
                    pe.wait_ge(x2T_read, B)
                if k >= 6:
                    pe.wait_ge(h_out, k - 5)
                mm(ps[:, k % 6, :], wT[:, k // (B * NI), kk % NI, :], xq[:, kk // NI, :], start=True, stop=True)\
                    .then_inc(h_filled, 1)
                if k == B * NI + 3:
                    turn_max(1)
            for n in range(2, 5):
                turn_max(n)
            pe.wait_ge(h_out, 2 * B * NI)
            warm_up(5, 10)
            for b in range(B):
                pe.wait_ge(oq_made, b + 1)
                for t in range(NT):
                    for i in range(NI):
                        last = mm(ps[:, b, P * t:P * (t + 1)], up[:, b, i * T + P * t:i * T + P * (t + 1)], wT[:, 2, i, :],
                                  start=(i == 0), stop=(i == NI - 1))
                last.then_inc(down_filled, 1)


def tables():
    f = np.concatenate([np.arange(T // 2 + 1), np.arange(1, T // 2)])
    angle = 2 * np.pi * ((f[None, :] * np.arange(T)[:, None]) % T) / T
    cosines = np.arange(T) <= T // 2
    forward = np.where(cosines[None, :], np.cos(angle), np.sin(angle))
    twice = np.where((f == 0) | (f == T // 2), 1.0, 2.0)
    inverse = (forward * twice[None, :] / T / C).T
    parts = np.array([[n != 0, n == 2] for _ in range(D) for n in K_PART])
    return forward.astype(np.float32), np.ascontiguousarray(inverse.astype(np.float32)), parts.astype(np.float32)


def kernel(x, ctx_1024, L0_attn_Wk, L0_attn_Wv, L0_attn_Wq, L0_attn_Wp, L0_attn_bp, L0_xattn_Wq, L0_xattn_bq, L0_xattn_Wk,
           L0_xattn_bk, L0_xattn_Wv, L0_xattn_bv, L0_xattn_Wo, L0_xattn_bo, L0_ffn_w_gate, L0_ffn_w_up, L0_ffn_w_down):
    import concourse.bacc as bacc
    from concourse.bass_utils import run_bass_kernel_spmd

    dft, idft, parts = tables()
    def cat(*arrays):
        return np.concatenate([np.asarray(a) for a in arrays], axis=1)

    def by_rows(w):
        return np.asarray(w).reshape(NI, P, C).transpose(1, 0, 2).reshape(P, NI * C)

    given = {
        "x": x, "xT": np.asarray(x).reshape(B * T, C).T,
        "qkv": cat(np.asarray(L0_attn_Wq).transpose(1, 0, 2).reshape(C, NH * D), L0_attn_Wk, L0_attn_Wv),
        "weights": cat(L0_attn_Wp, np.asarray(L0_xattn_Wq).T, L0_xattn_Wk, L0_xattn_Wv, L0_xattn_Wo),
        "ctxT": np.asarray(ctx_1024).transpose(2, 0, 1),
        "col_bias": np.stack([np.asarray(L0_xattn_bq), np.asarray(L0_xattn_bv)], axis=1),
        "row_bias": np.stack([np.asarray(L0_attn_bp), np.asarray(L0_xattn_bo), np.asarray(L0_xattn_bk)]),
        "ffn": cat(by_rows(L0_ffn_w_gate), by_rows(L0_ffn_w_up), L0_ffn_w_down),
        "dft": dft, "idft": idft, "parts": parts,
    }
    nc = bacc.Bacc("TRN2", target_bir_lowering=False, num_devices=1)
    arrays, args = {}, []
    for name, a in given.items():
        a = np.ascontiguousarray(a)
        arrays[f"in_{name}_dram"] = a
        args.append(nc.dram_tensor(f"in_{name}_dram", a.shape, mybir.dt.from_np(a.dtype), kind="ExternalInput").ap())
    args.append(nc.dram_tensor("out_0_dram", (B, T, C), F32, kind="ExternalOutput").ap())
    decoder_layer(nc, *args)
    r = run_bass_kernel_spmd(nc, [arrays], core_ids=[0])
    return r.results[0]["out_0_dram"]
```
